# Optimizing a Trainium2 kernel written in Bass

```python
import numpy as np
import jax
import jax.numpy as jnp

def _softmax(x, axis=-1):
    return jax.nn.softmax(x, axis=axis)

def _gelu(x):
    return jax.nn.gelu(x, approximate=True)

def _silu(x):
    return jax.nn.silu(x)

def _sigmoid(x):
    return jax.nn.sigmoid(x)

def _layernorm(x, axis=-1, eps=1e-05):
    m = jnp.mean(x, axis=axis, keepdims=True)
    v = jnp.var(x, axis=axis, keepdims=True)
    return (x - m) / jnp.sqrt(v + eps)

def _scatter_add(tgt, idx, src, axis=0):
    return tgt.at[idx].add(src)

def _segment_sum(src, seg, n):
    return jax.ops.segment_sum(src, seg, n)
kernel_name = 'mk_seq_postln_d1_jaxref_r8_5b0756'

def setup_inputs(seed: int=0):
    np.random.seed(seed)
    _w = jnp.asarray

    def _L0_attn_setup():
        import jax, jax.numpy as jnp
        import numpy as np
        import math
        D_MODEL, D_C, D_R, NH = (128, 128, 32, 16)
        HD = D_MODEL // NH
        B, T = (2, 256)

        def _rope_tables(T, d_R):
            inv_freq = 1.0 / 10000.0 ** (jnp.arange(0, d_R, 2, dtype=jnp.float32) / d_R)
            t = jnp.arange(T, dtype=jnp.float32)
            freqs = jnp.outer(t, inv_freq)
            return (jnp.cos(freqs), jnp.sin(freqs))

        def _rotary_apply(x, cos, sin):
            d = x.shape[-1]
            x1, x2 = (x[..., :d // 2], x[..., d // 2:])
            return jnp.concatenate([x1 * cos - x2 * sin, x2 * cos + x1 * sin], axis=-1)
        key = jax.random.key(seed)
        ks = jax.random.split(key, 8)
        s = lambda fan_in: 1.0 / math.sqrt(fan_in)
        return {'x': jax.random.normal(ks[0], (B, T, D_MODEL), jnp.float32), 'W_kv_down': jax.random.normal(ks[1], (D_MODEL, D_C), jnp.float32) * s(D_MODEL), 'W_k_up': jax.random.normal(ks[2], (D_C, D_MODEL), jnp.float32) * s(D_C), 'W_v_up': jax.random.normal(ks[3], (D_C, D_MODEL), jnp.float32) * s(D_C), 'W_q': jax.random.normal(ks[4], (D_MODEL, D_MODEL), jnp.float32) * s(D_MODEL), 'W_q_rope': jax.random.normal(ks[5], (D_MODEL, D_R), jnp.float32) * s(D_MODEL), 'W_k_rope': jax.random.normal(ks[6], (D_C, D_R), jnp.float32) * s(D_C), 'W_o': jax.random.normal(ks[7], (D_MODEL, D_MODEL), jnp.float32) * s(D_MODEL)}
    _L0_attn_in = _L0_attn_setup()

    def _L0_ffn_setup():
        import jax, jax.numpy as jnp
        import numpy as np
        TOP_K = 2

        def _gelu(x):
            return jax.nn.gelu(x, approximate=False)
        key = jax.random.key(seed)
        ks = jax.random.split(key, 6)
        B, S, D, F, E = (2, 256, 128, 256, 8)
        sc_g = 1.0 / np.sqrt(D)

        def xav(k, shape, fan_in, fan_out):
            lim = np.sqrt(6.0 / (fan_in + fan_out))
            return jax.random.uniform(k, shape, jnp.float32, -lim, lim)
        return {'x': jax.random.normal(ks[0], (B, S, D), jnp.float32), 'Wg': xav(ks[1], (D, E), D, E), 'Wu': xav(ks[2], (E, D, F), D, F), 'Wd': xav(ks[3], (E, F, D), F, D), 'W1': xav(ks[4], (D, F), D, F), 'W2': xav(ks[5], (F, D), F, D)}
    _L0_ffn_in = _L0_ffn_setup()
    _d = {'L0_attn_x': _L0_attn_in['x'], 'L0_attn_W_kv_down': _L0_attn_in['W_kv_down'], 'L0_attn_W_k_up': _L0_attn_in['W_k_up'], 'L0_attn_W_v_up': _L0_attn_in['W_v_up'], 'L0_attn_W_q': _L0_attn_in['W_q'], 'L0_attn_W_q_rope': _L0_attn_in['W_q_rope'], 'L0_attn_W_k_rope': _L0_attn_in['W_k_rope'], 'L0_attn_W_o': _L0_attn_in['W_o'], 'L0_ffn_Wg': _L0_ffn_in['Wg'], 'L0_ffn_Wu': _L0_ffn_in['Wu'], 'L0_ffn_Wd': _L0_ffn_in['Wd'], 'L0_ffn_W1': _L0_ffn_in['W1'], 'L0_ffn_W2': _L0_ffn_in['W2']}
    _x0 = _d['L0_attn_x']
    _d['L0_attn_x'] = jax.random.normal(jax.random.fold_in(jax.random.key(seed), 1), (32, 256, 128), dtype=_x0.dtype)
    del _x0
    return _d

def reference(L0_attn_x, L0_attn_W_kv_down, L0_attn_W_k_up, L0_attn_W_v_up, L0_attn_W_q, L0_attn_W_q_rope, L0_attn_W_k_rope, L0_attn_W_o, L0_ffn_Wg, L0_ffn_Wu, L0_ffn_Wd, L0_ffn_W1, L0_ffn_W2):

    def _L0_attn_ref(x, W_kv_down, W_k_up, W_v_up, W_q, W_q_rope, W_k_rope, W_o):
        import jax, jax.numpy as jnp
        import numpy as np
        import math
        D_MODEL, D_C, D_R, NH = (128, 128, 32, 16)
        HD = D_MODEL // NH
        B, T = (2, 256)

        def _rope_tables(T, d_R):
            inv_freq = 1.0 / 10000.0 ** (jnp.arange(0, d_R, 2, dtype=jnp.float32) / d_R)
            t = jnp.arange(T, dtype=jnp.float32)
            freqs = jnp.outer(t, inv_freq)
            return (jnp.cos(freqs), jnp.sin(freqs))

        def _rotary_apply(x, cos, sin):
            d = x.shape[-1]
            x1, x2 = (x[..., :d // 2], x[..., d // 2:])
            return jnp.concatenate([x1 * cos - x2 * sin, x2 * cos + x1 * sin], axis=-1)
        Bb, Tt, _ = x.shape
        cos, sin = _rope_tables(Tt, D_R)
        cos = cos[None]
        sin = sin[None]
        c_kv = x @ W_kv_down
        k_rope = _rotary_apply(c_kv @ W_k_rope, cos, sin)
        k = (c_kv @ W_k_up).reshape(Bb, Tt, NH, HD)
        v = (c_kv @ W_v_up).reshape(Bb, Tt, NH, HD)
        q = (x @ W_q).reshape(Bb, Tt, NH, HD)
        q_rope = _rotary_apply(x @ W_q_rope, cos, sin)
        scale = math.sqrt(HD + D_R)
        scores = jnp.einsum('bqhd,bkhd->bhqk', q, k)
        scores = scores + jnp.einsum('bqr,bkr->bqk', q_rope, k_rope)[:, None]
        scores = scores / scale
        causal = jnp.triu(jnp.ones((Tt, Tt), dtype=bool), k=1)
        scores = jnp.where(causal[None, None], -jnp.inf, scores)
        w = jax.nn.softmax(scores, axis=-1)
        attn = jnp.einsum('bhqk,bkhd->bqhd', w, v).reshape(Bb, Tt, D_MODEL)
        return attn @ W_o

    def _L0_ffn_ref(x, Wg, Wu, Wd, W1, W2):
        import jax, jax.numpy as jnp
        import numpy as np
        TOP_K = 2

        def _gelu(x):
            return jax.nn.gelu(x, approximate=False)
        B, S, D = x.shape
        E = Wu.shape[0]
        T = B * S
        xt = x.reshape(T, D)
        probs = jax.nn.softmax(xt @ Wg, axis=-1)
        topv, topi = jax.lax.top_k(probs, TOP_K)
        topv = topv / jnp.sum(topv, axis=-1, keepdims=True)
        cw = jnp.zeros((T, E), x.dtype).at[jnp.arange(T)[:, None], topi].set(topv)
        h = _gelu(jnp.einsum('td,edf->tef', xt, Wu))
        y = jnp.einsum('tef,efd->ted', h, Wd)
        moe = jnp.einsum('ted,te->td', y, cw)
        shared = _gelu(xt @ W1) @ W2
        return (shared + moe).reshape(B, S, D)
    x = L0_attn_x
    x = _layernorm(x + _L0_attn_ref(x, L0_attn_W_kv_down, L0_attn_W_k_up, L0_attn_W_v_up, L0_attn_W_q, L0_attn_W_q_rope, L0_attn_W_k_rope, L0_attn_W_o), axis=-1)
    x = _layernorm(x + _L0_ffn_ref(x, L0_ffn_Wg, L0_ffn_Wu, L0_ffn_Wd, L0_ffn_W1, L0_ffn_W2), axis=-1)
    return x

_drawn_inputs = setup_inputs


def setup_inputs(seed=0):
    import zlib

    import numpy as np

    out = dict(_drawn_inputs(seed))
    spreads = {}
    factors = {}
    for name, (base, spread) in spreads.items():
        noise = np.random.default_rng([zlib.crc32(name.encode()), seed]).standard_normal(out[name].shape)
        drawn = base * np.exp(spread * noise) if base else spread * noise
        out[name] = jnp.asarray(drawn.astype(out[name].dtype))
    for name, factor in factors.items():
        out[name] = (out[name] * factor).astype(out[name].dtype)
    return out
```

```python
from contextlib import ExitStack

import numpy as np

import concourse.bass as bass
from concourse import mybir

ALU = mybir.AluOpType
ACT = mybir.ActivationFunctionType
F32 = mybir.dt.float32
F16 = mybir.dt.float16
BF16 = mybir.dt.bfloat16
U32 = mybir.dt.uint32
AX_X = mybir.AxisListType.X

P = 128
NB, T, D = 32, 256, 128
NT = T // P
NH, HD, DR = 16, 8, 32
NE, F = 8, 256
NF = F // P
NX = NE + 1
EPS = 1e-5
SCORE_SCALE = 1.0 / float(np.sqrt(HD + DR))
X_SCALE, W_SCALE = 16.0, 64.0
UNSCALE = 1.0 / (X_SCALE * W_SCALE)
ROPE_ROWS = 3 * DR
QK_ROWS = ROPE_ROWS + 3 * HD
STACK_ROWS = QK_ROWS + 2
QUADS = [[3 * j + i for j in range(4)] for i in range(3)] + [[12 + j for j in range(4)]]
SUMCOL = HD
P_RING = 6
SLOTS = 12
DOWN_IN_SLOT = [2, 2, 1, 2, 1, 1]
UP_IN_SLOT = [2, 1, 2, 1, 2, 1]
MAX_IN_SLOT = [2, 2, 3, 3, 2]
N_GROUPS = 12
N_AV = 8
NEG = -1e30
MAX_GROUPS = [(0, 4 * g, 4) for g in range(4)] + [(1, 2 * g, 2) for g in range(8)]
LOOP_FROM, LOOP_TO = 6, 30


class Batch:

    def __init__(self, index, pair, parity, exists=True):
        self.index, self.pair, self.parity, self.exists = index, pair, parity, exists

    def count(self, per_batch, j=0):
        return self.index * per_batch + j

    def before(self, k):
        return Batch(self.index - k, None, (self.parity + k) % 2)


def walk(engine, iteration):

    def plain(i):
        def at(offset):
            n = i + offset
            return Batch(n, n // 2, n % 2, 0 <= n < NB)
        iteration(at)

    def looped(k, half):
        def at(offset):
            n = half + offset
            return Batch(2 * k + n, k + n // 2, n % 2)
        iteration(at)

    for i in range(-2, LOOP_FROM):
        plain(i)
    with engine.Fori(LOOP_FROM // 2, LOOP_TO // 2) as k:
        looped(k, 0)
        looped(k, 1)
    for i in range(LOOP_TO, NB + 3):
        plain(i)


def wait(engine, semaphore, value):
    if not isinstance(value, int) or value > 0:
        engine.wait_ge(semaphore, value)


def wait_before(engine, semaphore, value, passed):
    engine.wait_ge(semaphore, value)
    engine.sem_inc(passed, 1)


def av_of_group(g):
    return g // 2 if g < 8 else g - 4


def build_layer(nc, x, w_kvd, w_ku, w_vu, w_q, w_qr, w_kr, w_o, w_g, w_u, w_d, w_1, w_2, tables, out):
    ctx = ExitStack()
    with ctx:
        def sb(name, shape, dt=F32):
            return ctx.enter_context(nc.sbuf_tensor(name, shape, dt))

        def ps(name, shape):
            return ctx.enter_context(nc.psum_tensor(name, shape, F32))

        def sem(name):
            return ctx.enter_context(nc.semaphore(name))

        wkvd = sb("wkvd", [P, D])
        wv = sb("wv", [P, D])
        wo = sb("wo", [P, D])
        wq_in = sb("wq_in", [P, D])
        wk_in = sb("wk_in", [P, D])
        wqr_in = sb("wqr_in", [P, DR])
        wkr_in = sb("wkr_in", [P, DR])
        wg_in = sb("wg_in", [P, NE])
        wu_in = sb("wu_in", [P, NX, F])
        wd = sb("wd", [P, NX, NF, D])
        rope = sb("rope", [ROPE_ROWS, 2, T])
        wq = sb("wq", [P, HD, NH])
        wk = sb("wk", [P, HD, NH])
        wqr = sb("wqr", [P, 3, DR])
        wkr = sb("wkr", [P, 3, DR])
        wqr_swap = sb("wqr_swap", [P, 3, DR])
        wkr_swap = sb("wkr_swap", [P, 3, DR])
        wg_hi = sb("wg_hi", [P, NE], F16)
        wg_lo = sb("wg_lo", [P, NE], F16)
        wu_hi = sb("wu_hi", [P, NX, F], F16)
        wu_lo = sb("wu_lo", [P, NX, F], F16)
        ident = sb("ident", [P, P])
        ident_bf = sb("ident_bf", [P, P], BF16)
        causal = sb("causal", [P, 4, P], BF16)
        lo_rows_q = sb("lo_rows_q", [P, 1])
        lo_rows_k = sb("lo_rows_k", [P, 1])
        minus_half = sb("minus_half", [P, NT])
        expert_no = sb("expert_no", [P, NE])
        expert_int = sb("expert_int", [P, NE], mybir.dt.int32)
        xin = sb("xin", [P, 2, NT, D])
        xT = sb("xT", [P, 2, T])
        ckvT = sb("ckvT", [P, 2, T])
        qk_hi = sb("qk_hi", [P, 2, T], F16)
        qk_lo = sb("qk_lo", [P, 2, T], F16)
        rope_cos = sb("rope_cos", [ROPE_ROWS, 2, T])
        rope_sin = sb("rope_sin", [ROPE_ROWS, 2, T])
        rope_sum = sb("rope_sum", [ROPE_ROWS, 2, T])
        rope_hi = sb("rope_hi", [ROPE_ROWS, 2, T], F16)
        rope_st = sb("rope_st", [ROPE_ROWS, 2, T], F16)
        q_st = sb("q_st", [P, 2, NH, T], F16)
        k_st = sb("k_st", [P, 2, NH, T], F16)
        v_pad = sb("v_pad", [P, 2, NT, NH, 32])
        neg_max = sb("neg_max", [P, NT, NH])
        nm_hi = sb("nm_hi", [NH, T], F16)
        nm_lo = sb("nm_lo", [NH, T], F16)
        probs = sb("probs", [P, P_RING, 512])
        av_sb = sb("av_sb", [P, 2, T])
        sum_inv = sb("sum_inv", [P, NT, NH])
        attn = sb("attn", [P, NT, D])
        attnT = sb("attnT", [P, T])
        xres = sb("xres", [P, 2, NT, D])
        res1 = sb("res1", [P, NT, D])
        stats1 = sb("stats1", [P, NT, 6])
        mv1 = sb("mv1", [P, NT, 2])
        ve1 = sb("ve1", [P, NT])
        rstd1 = sb("rstd1", [P, NT])
        x1 = sb("x1", [P, 2, NT, D])
        x1_hi = sb("x1_hi", [P, 2, T], F16)
        x1_lo = sb("x1_lo", [P, 2, T], F16)
        top = sb("top", [P, 2, NT, 8])
        top_at = sb("top_at", [P, 2, NT, 8], U32)
        logits = sb("logits", [P, NT, NE])
        gap = sb("gap", [P, 2, NT])
        gap_exp = sb("gap_exp", [P, NT])
        top_no = sb("top_no", [P, NT, 8])
        gate_den = sb("gate_den", [P, NT])
        gate1 = sb("gate1", [P, NT])
        gate2 = sb("gate2", [P, NT])
        pick1 = sb("pick1", [P, NT, NE])
        pick2 = sb("pick2", [P, NT, NE])
        gates = sb("gates", [P, 2, NT, NE])
        hid = sb("hid", [P, NX, NF, T])
        acc = sb("acc", [P, NT, D])
        stats2 = sb("stats2", [P, NT, 6])
        mv2 = sb("mv2", [P, NT, 2])
        ve2 = sb("ve2", [P, NT])
        rstd2 = sb("rstd2", [P, NT])
        yout = sb("yout", [P, 2, NT, D])

        ring = ps("ring", [P, 3, 512])
        mbank = ps("mbank", [P, 2, 512])
        avbank = ps("avbank", [P, 2, T])
        xbank = ps("xbank", [P, 512])
        ybank = ps("ybank", [P, 512])

        ld_w = sem("ld_w")
        consts_made = sem("consts_made")
        weights_made = sem("weights_made")
        ld_x = [sem("ld_x0"), sem("ld_x1")]
        ld_r = [sem("ld_r0"), sem("ld_r1")]
        st_qk = sem("st_qk")
        st_rope = sem("st_rope")
        st_max = sem("st_max")
        st_out = [sem("st_out0"), sem("st_out1")]
        pe_xT = sem("pe_xT")
        pe_ckv = sem("pe_ckv")
        pe_qk = sem("pe_qk")
        pe_rope = sem("pe_rope")
        pe_swap = sem("pe_swap")
        pe_v = sem("pe_v")
        pe_max = sem("pe_max")
        pe_nmT = sem("pe_nmT")
        pe_score = sem("pe_score")
        pe_av = sem("pe_av")
        pe_avT = sem("pe_avT")
        pe_attnT = sem("pe_attnT")
        pe_o = sem("pe_o")
        pe_x1T = sem("pe_x1T")
        pe_logit = sem("pe_logit")
        pe_up = sem("pe_up")
        pe_down = sem("pe_down")
        act_xT = sem("act_xT")
        act_ckv = sem("act_ckv")
        act_qk_hi = sem("act_qk_hi")
        act_exp = sem("act_exp")
        act_av = sem("act_av")
        act_attnT = sem("act_attnT")
        act_x1_hi = sem("act_x1_hi")
        act_gap = sem("act_gap")
        act_gelu = sem("act_gelu")
        pool_mask = sem("pool_mask")
        pool_rstd1 = sem("pool_rstd1")
        pool_rstd2 = sem("pool_rstd2")
        pool_passed = sem("pool_passed")
        dve_passed = sem("dve_passed")
        dve_qk_lo = sem("dve_qk_lo")
        dve_rope = sem("dve_rope")
        dve_v = sem("dve_v")
        dve_norm = sem("dve_norm")
        dve_ln1 = sem("dve_ln1")
        dve_x1_lo = sem("dve_x1_lo")
        dve_route = sem("dve_route")
        dve_gate = sem("dve_gate")
        dve_max = sem("dve_max")
        dve_nm = sem("dve_nm")
        dve_sum = sem("dve_sum")
        dve_ln2 = sem("dve_ln2")
        CONSTS, WEIGHTS = 12, 14
        N_ROPE, N_V, N_NORM, N_LN, N_ROUTE, N_GATE = 6, 3, 5, 7, 6, 9
        N_SUM = 1 + NE * NT

        x_tiles = x.rearrange("b (t p) d -> b p t d", p=P)
        out_tiles = out.rearrange("b (t p) d -> b p t d", p=P)

        def dram_batch(ap, batch):
            return ap[bass.ds(batch.index, 1)].rearrange("b p t d -> (b p) t d")

        weight_loads = [
            (wkvd[:, :], w_kvd), (wq_in[:, :], w_q), (wk_in[:, :], w_ku), (wqr_in[:, :], w_qr),
            (wkr_in[:, :], w_kr), (rope[:, :, :], tables), (wv[:, :], w_vu), (wo[:, :], w_o),
            (wg_in[:, :], w_g), (wu_in[:, 0, :], w_1),
            (wu_in[:, 1:NX, :], w_u.rearrange("e p f -> p e f")),
            (wd[:, 0, :, :], w_2.rearrange("(c p) d -> p c d", p=P)),
            (wd[:, 1:NX, :, :], w_d.rearrange("e (c p) d -> p e c d", p=P)),
        ]
        ALL_WEIGHTS = 16 * len(weight_loads)

        block = ctx.enter_context(nc.Block())

        @block.sync
        def _(sp):
            for to, source in weight_loads:
                sp.dma_start(to, source).then_inc(ld_w, 16)

            def load_x(n):
                wait(sp, pe_xT, n.count(1, -1))
                sp.dma_start(xin[:, n.parity], dram_batch(x_tiles, n)).then_inc(ld_x[n.parity], 16)

            def load_residual(n):
                wait(sp, dve_ln1, n.count(N_LN, 1 - 2 * N_LN))
                sp.dma_start(xres[:, n.parity], dram_batch(x_tiles, n)).then_inc(ld_r[n.parity], 16)

            def stack_heads(n):
                wait(sp, pe_score, n.count(N_GROUPS, -N_GROUPS))
                wait(sp, act_qk_hi, n.count(1, 1))
                wait(sp, dve_qk_lo, n.count(1, 1))
                for j, (q_part, k_part) in enumerate([(qk_hi, qk_hi), (qk_hi, qk_lo), (qk_lo, qk_hi)]):
                    rows = slice(ROPE_ROWS + j * HD, ROPE_ROWS + (j + 1) * HD)
                    sp.dma_start(q_st[rows, n.parity], q_part[:, 0, :]).then_inc(st_qk, 16)
                    sp.dma_start(k_st[rows, n.parity], k_part[:, 1, :]).then_inc(st_qk, 16)

            def stack_rope(n):
                wait(sp, dve_rope, n.count(N_ROPE, N_ROPE))
                for j, stack in enumerate([q_st, k_st]):
                    src = rope_st[:, j, :].unsqueeze(1).to_broadcast([ROPE_ROWS, NH, T])
                    sp.dma_start(stack[0:ROPE_ROWS, n.parity], src).then_inc(st_rope, 16)

            def stack_max(n):
                wait(sp, dve_nm, n.count(2, 2))
                for j, part in enumerate([nm_hi, nm_lo]):
                    row = slice(QK_ROWS + j, QK_ROWS + j + 1)
                    sp.dma_start(q_st[row, n.parity], part[:, :]).then_inc(st_max, 16)

            def store(n):
                wait(sp, dve_ln2, n.count(N_LN - 1, N_LN - 1))
                sp.dma_start(dram_batch(out_tiles, n), yout[:, n.parity]).then_inc(st_out[n.parity], 16)

            def iteration(at):
                if at(2).exists:
                    load_x(at(2))
                if at(-1).exists:
                    load_residual(at(-1))
                if at(1).exists:
                    stack_heads(at(1))
                    stack_rope(at(1))
                if at(-3).exists:
                    store(at(-3))
                if at(1).exists:
                    stack_max(at(1))

            sp.wait_ge(consts_made, 2)
            walk(sp, iteration)
            for parity in range(2):
                sp.wait_ge(st_out[parity], 16 * NB // 2)

        @block.tensor
        def _(pe):
            def transpose_x(n):
                pe.wait_ge(ld_x[n.parity], n.pair * 16 + 16)
                for t in range(NT):
                    mm = pe.transpose(xbank[:, t * P:(t + 1) * P], xin[:, n.parity, t, :], ident[:, :])
                mm.then_inc(pe_xT, 1)

            def down_project(n):
                pe.wait_ge(act_xT, n.count(1, 1))
                pe.matmul(xbank[:, 0:T], wkvd[:, :], xT[:, n.parity, :], start=True, stop=True
                          ).then_inc(pe_ckv, 1)

            def project_qk(n):
                pe.wait_ge(act_ckv, n.count(1, 1))
                wait(pe, dve_nm, n.count(2, 0))
                pe.matmul(xbank[:, 0:T], wq[:, :, :].rearrange("p d h -> p (d h)"), xT[:, n.parity, :],
                          start=True, stop=True)
                pe.matmul(xbank[:, T:2 * T], wk[:, :, :].rearrange("p d h -> p (d h)"), ckvT[:, n.parity, :],
                          start=True, stop=True).then_inc(pe_qk, 1)

            def project_rope(n, w_of_q, w_of_k, done):
                pe.matmul(xbank[0:ROPE_ROWS, 0:T], w_of_q[:, :, :].rearrange("p a r -> p (a r)"),
                          xT[:, n.parity, :], start=True, stop=True)
                pe.matmul(xbank[0:ROPE_ROWS, T:2 * T], w_of_k[:, :, :].rearrange("p a r -> p (a r)"),
                          ckvT[:, n.parity, :], start=True, stop=True).then_inc(done, 1)

            def project_v(n):
                for t in range(NT):
                    mm = pe.matmul(xbank[:, t * P:(t + 1) * P], ckvT[:, n.parity, t * P:(t + 1) * P], wv[:, :],
                                   start=True, stop=True)
                mm.then_inc(pe_v, 1)

            def max_group(n, g):
                if g == 0:
                    pe.wait_ge(st_qk, n.count(96, 96))
                    pe.wait_ge(st_rope, n.count(32, 32))
                wait(pe, dve_max, n.count(N_GROUPS, g - 1))
                t, h0, nh = MAX_GROUPS[g]
                keys = (t + 1) * P
                bank = mbank[:, g % 2, :].rearrange("p (h k) -> p h k", h=nh)
                pe.matmul(bank[:, :, t * P:keys], ident_bf[:, :], causal[:, 0:nh, :],
                          start=True, stop=False, skip_group_check=True)
                for a in range(nh):
                    mm = pe.matmul(bank[:, a, :], q_st[0:QK_ROWS, n.parity, h0 + a, t * P:keys],
                                   k_st[0:QK_ROWS, n.parity, h0 + a, 0:keys],
                                   start=False, stop=(a == nh - 1), skip_group_check=True)
                mm.then_inc(pe_max, 1)

            def transpose_max(n):
                pe.wait_ge(dve_max, n.count(N_GROUPS, N_GROUPS))
                for t in range(NT):
                    mm = pe.transpose(xbank[0:NH, t * P:(t + 1) * P], neg_max[:, t, :], ident[:, :])
                mm.then_inc(pe_nmT, 1)

            def score_group(n, g, up_before):
                if g == 0:
                    pe.wait_ge(st_max, n.count(32, 32))
                    pe.wait_ge(dve_v, n.count(N_V, N_V))
                if g >= 3:
                    pe.wait_ge(act_exp, n.count(N_GROUPS, g - 2))
                elif up_before.exists:
                    pe.wait_ge(act_gelu, up_before.count(NX, NX - 2 + g))
                else:
                    wait(pe, act_exp, n.count(N_GROUPS, g - 2))
                if g < 8:
                    heads, kt = QUADS[g // 2][2 * (g % 2):2 * (g % 2) + 2], 0
                else:
                    heads, kt = QUADS[g - 8], 1
                width = T - kt * P
                for a, h in enumerate(heads):
                    mm = pe.matmul(ring[:, g % 3, a * width:(a + 1) * width],
                                   k_st[0:STACK_ROWS, n.parity, h, kt * P:(kt + 1) * P],
                                   q_st[0:STACK_ROWS, n.parity, h, kt * P:T], start=True, stop=True)
                mm.then_inc(pe_score, 1)

            def values_step(n, s):
                groups = [2 * s, 2 * s + 1] if s < 4 else [s + 4]
                pe.wait_ge(pool_mask, n.count(N_GROUPS, groups[-1] + 1))
                if s == 0:
                    wait(pe, act_av, n.count(1, 0))
                kt, quad = s // 4, s % 4
                part, cols = quad // 3, slice(kt * P, T)
                for j, h in enumerate(QUADS[quad]):
                    if kt == 0:
                        p_cols = probs[:, groups[j // 2] % P_RING, (j % 2) * T:(j % 2 + 1) * T]
                    else:
                        p_cols = probs[:, groups[0] % P_RING, j * P:(j + 1) * P]
                    mm = pe.matmul(avbank[32 * j:32 * j + 32, part, cols], v_pad[:, n.parity, kt, h, :], p_cols,
                                   start=(s == 0), stop=(s == N_AV - 1), skip_group_check=True,
                                   tile_position=(0, 32 * j))
                mm.then_inc(pe_av, 1)

            def transpose_av(n):
                pe.wait_ge(act_av, n.count(1, 1))
                for part in range(2):
                    for t in range(NT):
                        mm = pe.transpose(xbank[:, (part * NT + t) * P:(part * NT + t + 1) * P],
                                          av_sb[:, part, t * P:(t + 1) * P], ident[:, :])
                mm.then_inc(pe_avT, 1)

            def transpose_attn(n):
                pe.wait_ge(dve_norm, n.count(N_NORM, N_NORM))
                for t in range(NT):
                    mm = pe.transpose(xbank[:, t * P:(t + 1) * P], attn[:, t, :], ident[:, :])
                mm.then_inc(pe_attnT, 1)

            def project_out(n):
                pe.wait_ge(act_attnT, n.count(1, 1))
                for t in range(NT):
                    mm = pe.matmul(xbank[:, t * P:(t + 1) * P], attnT[:, t * P:(t + 1) * P], wo[:, :],
                                   start=True, stop=True)
                mm.then_inc(pe_o, 1)

            def transpose_x1(n):
                pe.wait_ge(dve_ln1, n.count(N_LN, N_LN))
                for t in range(NT):
                    mm = pe.transpose(xbank[:, t * P:(t + 1) * P], x1[:, n.parity, t, :], ident[:, :])
                mm.then_inc(pe_x1T, 1)

            def router(n):
                pe.wait_ge(dve_x1_lo, n.count(1, 1))
                for t in range(NT):
                    terms = [(x1_hi, wg_hi), (x1_lo, wg_hi), (x1_hi, wg_lo)]
                    for j, (xp, wp) in enumerate(terms):
                        mm = pe.matmul(xbank[:, t * NE:(t + 1) * NE], xp[:, n.parity, t * P:(t + 1) * P], wp[:, :],
                                       start=(j == 0), stop=(j == 2))
                mm.then_inc(pe_logit, 1)

            def up(n, e, attending):
                if e >= 3:
                    pe.wait_ge(act_gelu, n.count(NX, e - 2))
                elif attending.exists:
                    pe.wait_ge(act_exp, attending.count(N_GROUPS, N_GROUPS - 2 + e))
                else:
                    wait(pe, act_gelu, n.count(NX, e - 2))
                for c in range(NF):
                    terms = [(wu_hi, x1_hi), (wu_hi, x1_lo), (wu_lo, x1_hi)]
                    for j, (wp, xp) in enumerate(terms):
                        mm = pe.matmul(ring[:, e % 3, c * T:(c + 1) * T], wp[:, e, c * P:(c + 1) * P],
                                       xp[:, n.parity, :], start=(j == 0), stop=(j == 2))
                mm.then_inc(pe_up, 1)

            def down(n, e):
                pe.wait_ge(act_gelu, n.count(NX, e + 1))
                if e == 0:
                    wait(pe, dve_sum, n.count(N_SUM, 0))
                else:
                    pe.wait_ge(dve_sum, n.count(N_SUM, 1 + NT * (e - 1)))
                for t in range(NT):
                    for c in range(NF):
                        mm = pe.matmul(ybank[:, t * D:(t + 1) * D], hid[:, e, c, t * P:(t + 1) * P], wd[:, e, c, :],
                                       start=(c == 0), stop=(c == NF - 1))
                mm.then_inc(pe_down, 1)

            def iteration(at):
                coming, front, here, post, ups, downs = at(2), at(1), at(0), at(-1), at(-2), at(-3)
                e_down = e_up = g_max = 0
                for slot in range(SLOTS):
                    if slot < 6 and downs.exists:
                        for _ in range(DOWN_IN_SLOT[slot]):
                            down(downs, e_down)
                            e_down += 1
                    if slot >= 6 and ups.exists:
                        for _ in range(UP_IN_SLOT[slot - 6]):
                            up(ups, e_up, here)
                            e_up += 1
                    if slot == 0 and front.exists:
                        project_qk(front)
                    if slot == 1 and front.exists:
                        pe.wait_ge(dve_qk_lo, front.count(1, 1))
                        project_rope(front, wqr, wkr, pe_rope)
                    if slot == 2 and front.exists:
                        pe.wait_ge(dve_rope, front.count(N_ROPE, 1))
                        project_rope(front, wqr_swap, wkr_swap, pe_swap)
                    if slot == 3 and post.exists:
                        if front.exists:
                            pe.wait_ge(dve_rope, front.count(N_ROPE, 2))
                        else:
                            pe.wait_ge(dve_nm, 2 * NB)
                            wait(pe, dve_route, post.count(N_ROUTE, 0))
                        transpose_av(post)
                    if slot == 4 and front.exists:
                        if post.exists:
                            pe.wait_ge(dve_norm, post.count(N_NORM, N_NORM))
                        else:
                            pe.wait_ge(dve_rope, front.count(N_ROPE, 2))
                        project_v(front)
                    if slot == 5 and post.exists:
                        if front.exists:
                            pe.wait_ge(dve_v, front.count(N_V, N_V))
                        transpose_attn(post)
                    if slot == 6 and coming.exists:
                        if post.exists:
                            pe.wait_ge(act_attnT, post.count(1, 1))
                        elif front.exists:
                            pe.wait_ge(dve_v, front.count(N_V, N_V))
                        transpose_x(coming)
                    if slot == 7 and post.exists:
                        if coming.exists:
                            pe.wait_ge(act_xT, coming.count(1, 1))
                        project_out(post)
                    if slot == 8 and coming.exists:
                        if post.exists:
                            pe.wait_ge(dve_ln1, post.count(N_LN, 1))
                        down_project(coming)
                    if slot == 9 and post.exists:
                        if coming.exists:
                            pe.wait_ge(act_ckv, coming.count(1, 1))
                        transpose_x1(post)
                    if slot == 10 and post.exists:
                        router(post)
                    if 6 <= slot < 11 and front.exists:
                        for _ in range(MAX_IN_SLOT[slot - 6]):
                            max_group(front, g_max)
                            g_max += 1
                    if slot == 11 and front.exists:
                        if post.exists:
                            pe.wait_ge(dve_route, post.count(N_ROUTE, 1))
                        elif coming.exists:
                            pe.wait_ge(act_ckv, coming.count(1, 1))
                        transpose_max(front)
                    if slot < 6 and here.exists:
                        score_group(here, 2 * slot, at(-3))
                        score_group(here, 2 * slot + 1, at(-3))
                    if here.exists:
                        if 1 <= slot <= 4:
                            values_step(here, slot - 1)
                        if slot == 5:
                            values_step(here, 4)
                            values_step(here, 5)
                        if slot == 6:
                            values_step(here, 6)
                            values_step(here, 7)

            pe.wait_ge(consts_made, CONSTS)
            pe.wait_ge(weights_made, WEIGHTS)
            pe.wait_ge(ld_w, ALL_WEIGHTS)
            walk(pe, iteration)

        @block.scalar
        def _(act):
            def copy_hi_qk(n):
                pe_done = n.count(1, 1)
                act.wait_ge(pe_qk, pe_done)
                wait(act, st_qk, n.count(96, 0))
                act.copy(qk_hi[:, :, :].rearrange("p a t -> p (a t)"), xbank[:, :]).then_inc(act_qk_hi, 1)

            def gap_exponential(n):
                act.wait_ge(dve_route, n.count(N_ROUTE, N_ROUTE))
                wait(act, dve_gate, n.count(N_GATE, 0))
                act.activation(gap_exp[:, :], gap[:, n.parity, :], ACT.Exp, scale=UNSCALE).then_inc(act_gap, 1)

            def exp_group(n, g):
                act.wait_ge(pe_score, n.count(N_GROUPS, g + 1))
                if g >= P_RING:
                    act.wait_ge(pe_av, n.count(N_AV, av_of_group(g - P_RING) + 1))
                else:
                    wait(act, pe_av, n.count(N_AV, av_of_group(g + P_RING) + 1 - N_AV))
                act.activation(probs[:, g % P_RING, :], ring[:, g % 3, :], ACT.Exp, scale=SCORE_SCALE
                               ).then_inc(act_exp, 1)

            def copy_av(n):
                act.wait_ge(pe_av, n.count(N_AV, N_AV))
                wait(act, pe_avT, n.count(1, 0))
                act.copy(av_sb[:, :, :], avbank[:, :, :]).then_inc(act_av, 1)

            def copy_attnT(n):
                act.wait_ge(pe_attnT, n.count(1, 1))
                wait(act, pe_o, n.count(1, 0))
                act.copy(attnT[:, :], xbank[:, 0:T]).then_inc(act_attnT, 1)

            def copy_xT(n):
                act.wait_ge(pe_xT, n.count(1, 1))
                wait(act, pe_swap, n.count(1, -1))
                act.copy(xT[:, n.parity, :], xbank[:, 0:T]).then_inc(act_xT, 1)

            def copy_ckv(n):
                act.wait_ge(pe_ckv, n.count(1, 1))
                wait(act, pe_v, n.count(1, -1))
                act.copy(ckvT[:, n.parity, :], xbank[:, 0:T]).then_inc(act_ckv, 1)

            def copy_hi_x1(n):
                act.wait_ge(pe_x1T, n.count(1, 1))
                wait(act, pe_up, n.count(NX, -NX))
                act.mul(x1_hi[:, n.parity, :], xbank[:, 0:T], X_SCALE).then_inc(act_x1_hi, 1)

            def gelu(n, e):
                act.wait_ge(pe_up, n.count(NX, e + 1))
                wait(act, pe_down, n.count(NX, e + 1 - NX))
                act.activation(hid[:, e, :, :].rearrange("p c t -> p (c t)"), ring[:, e % 3, :], ACT.Gelu,
                               scale=UNSCALE).then_inc(act_gelu, 1)

            def iteration(at):
                coming, front, here, post, ups = at(2), at(1), at(0), at(-1), at(-2)
                e_up = 0
                for slot in range(SLOTS):
                    if slot == 0 and ups.exists:
                        gap_exponential(ups)
                    if slot == 0 and front.exists:
                        copy_hi_qk(front)
                    if slot == 5 and post.exists:
                        copy_attnT(post)
                    if slot < 6 and here.exists:
                        exp_group(here, 2 * slot)
                        exp_group(here, 2 * slot + 1)
                    if slot == 6 and coming.exists:
                        copy_xT(coming)
                    if slot == 7 and here.exists:
                        copy_av(here)
                    if slot == 8 and coming.exists:
                        copy_ckv(coming)
                    if slot == 9 and post.exists:
                        copy_hi_x1(post)
                    if slot >= 6 and ups.exists:
                        for _ in range(UP_IN_SLOT[slot - 6]):
                            gelu(ups, e_up)
                            e_up += 1

            walk(act, iteration)

        @block.gpsimd
        def _(pool):
            pool.memset(q_st[:, :, :, :], 0.0).then_inc(consts_made, 1)
            pool.wait_ge(consts_made, 1)
            pool.memset(k_st[96:P, :, :, :], 1.0).then_inc(consts_made, 1)
            pool.wait_ge(consts_made, 2)
            pool.memset(ident[:, :], 0.0).then_inc(consts_made, 1)
            pool.wait_ge(consts_made, 3)
            pool.affine_select(out=ident[:, :], in_=ident[:, :], compare_op=ALU.not_equal, fill=1.0, base=0,
                               pattern=[[-1, P]], channel_multiplier=1).then_inc(consts_made, 1)
            pool.wait_ge(consts_made, 4)
            pool.memset(causal[:, :, :], 0.0).then_inc(consts_made, 1)
            pool.wait_ge(consts_made, 5)
            pool.affine_select(out=causal[:, :, :], in_=causal[:, :, :], compare_op=ALU.is_ge, fill=NEG, base=0,
                               pattern=[[0, 4], [-1, P]], channel_multiplier=1).then_inc(consts_made, 1)
            pool.wait_ge(consts_made, 6)
            pool.memset(lo_rows_q[:, :], 0.0).then_inc(consts_made, 1)
            pool.wait_ge(consts_made, 7)
            pool.memset(lo_rows_k[:, :], 0.0).then_inc(consts_made, 1)
            pool.wait_ge(consts_made, 8)
            pool.memset(lo_rows_q[2 * DR:3 * DR, :], -1.0).then_inc(consts_made, 1)
            pool.wait_ge(consts_made, 9)
            pool.memset(lo_rows_k[DR:2 * DR, :], -1.0).then_inc(consts_made, 1)
            pool.wait_ge(consts_made, 10)
            pool.memset(minus_half[:, :], -0.5).then_inc(consts_made, 1)
            pool.wait_ge(consts_made, 11)
            pool.iota(expert_int[:, :], pattern=[[1, NE]], base=0, channel_multiplier=0).then_inc(consts_made, 1)
            pool.wait_ge(consts_made, CONSTS)

            def mask_group(n, g):
                wait_before(pool, act_exp, n.count(N_GROUPS, g + 1), pool_passed)
                heads = 2 if g < 8 else 4
                block_of = probs[:, g % P_RING, :].rearrange("p (a q) -> p a q", a=heads)[:, :, 0:P]
                pool.affine_select(out=block_of, in_=block_of, compare_op=ALU.is_ge, fill=0.0, base=0,
                                   pattern=[[0, heads], [1, P]], channel_multiplier=-1).then_inc(pool_mask, 1)

            def inverse_deviation(n, made, mv, ve, rstd, done):
                wait_before(pool, made[0], made[1], pool_passed)
                pool.tensor_scalar(ve[:, :], mv[:, :, 1], EPS, None, ALU.add).then_inc(done, 1)
                pool.wait_ge(done, n.count(2, 1))
                pool.tensor_tensor(rstd[:, :], ve[:, :], minus_half[:, :], ALU.pow).then_inc(done, 1)

            def iteration(at):
                here, post, downs = at(0), at(-1), at(-3)
                for slot in range(SLOTS):
                    if slot < 6 and here.exists:
                        mask_group(here, 2 * slot)
                        mask_group(here, 2 * slot + 1)
                    if slot == 6 and downs.exists:
                        inverse_deviation(downs, (dve_ln2, downs.count(N_LN - 1, 4)), mv2, ve2, rstd2, pool_rstd2)
                    if slot == 8 and post.exists:
                        inverse_deviation(post, (dve_ln1, post.count(N_LN, 5)), mv1, ve1, rstd1, pool_rstd1)

            walk(pool, iteration)

        @block.vector
        def _(dve):
            dve.memset(v_pad[:, :, :, :, :], 0.0).then_inc(weights_made, 1)
            dve.wait_ge(weights_made, 1)
            for parity in range(2):
                for t in range(NT):
                    for quad, heads in enumerate(QUADS):
                        at_col = 9 * quad + SUMCOL if quad < 3 else SUMCOL
                        step = heads[1] - heads[0]
                        ones = dve.memset(v_pad[:, parity, t, heads[0]:heads[3] + 1:step, at_col:at_col + 1], 1.0)
            ones.then_inc(weights_made, 1)
            dve.wait_ge(ld_w, ALL_WEIGHTS)
            for w_in, w_to in [(wq_in, wq), (wk_in, wk)]:
                dve.tensor_copy(w_to[:, :, :], w_in[:, :].rearrange("p (h d) -> p d h", d=HD)
                                ).then_inc(weights_made, 1)
            for w_in, w_to, w_swap in [(wqr_in, wqr, wqr_swap), (wkr_in, wkr, wkr_swap)]:
                half = DR // 2
                dve.tensor_copy(w_to[:, :, :], w_in[:, :].unsqueeze(1).to_broadcast([P, 3, DR])
                                ).then_inc(weights_made, 1)
                dve.tensor_copy(w_swap[:, :, 0:half], w_in[:, half:DR].unsqueeze(1).to_broadcast([P, 3, half]))
                dve.tensor_copy(w_swap[:, :, half:DR], w_in[:, 0:half].unsqueeze(1).to_broadcast([P, 3, half])
                                ).then_inc(weights_made, 1)
            dve.tensor_scalar(wg_hi[:, :], wg_in[:, :], W_SCALE, None, ALU.mult).then_inc(weights_made, 1)
            dve.tensor_scalar(wu_hi[:, :, :], wu_in[:, :, :], W_SCALE, None, ALU.mult).then_inc(weights_made, 1)
            dve.wait_ge(weights_made, 10)
            dve.scalar_tensor_tensor(wg_lo[:, :], wg_in[:, :], W_SCALE, wg_hi[:, :], ALU.mult, ALU.subtract
                                     ).then_inc(weights_made, 1)
            dve.scalar_tensor_tensor(wu_lo[:, :, :], wu_in[:, :, :], W_SCALE, wu_hi[:, :, :],
                                     ALU.mult, ALU.subtract).then_inc(weights_made, 1)
            dve.wait_ge(consts_made, CONSTS)
            dve.tensor_copy(ident_bf[:, :], ident[:, :]).then_inc(weights_made, 1)
            dve.tensor_copy(expert_no[:, :], expert_int[:, :]).then_inc(weights_made, 1)
            dve.wait_ge(weights_made, WEIGHTS)

            def split_qk(n):
                dve.wait_ge(act_qk_hi, n.count(1, 1))
                wait(dve, st_qk, n.count(96, 0))
                dve.tensor_tensor(qk_lo[:, :, :].rearrange("p a t -> p (a t)"), xbank[:, :],
                                  qk_hi[:, :, :].rearrange("p a t -> p (a t)"), ALU.subtract).then_inc(dve_qk_lo, 1)

            def rope_products(n, made, table, to, j):
                dve.wait_ge(made, n.count(1, 1))
                of = xbank[0:ROPE_ROWS, :].rearrange("p (a t) -> p a t", a=2)
                dve.tensor_tensor(to[:, :, :], of, rope[:, table, :].unsqueeze(1).to_broadcast([ROPE_ROWS, 2, T]),
                                  ALU.mult).then_inc(dve_rope, 1)

            def rope_stacks(n):
                dve.wait_ge(dve_rope, n.count(N_ROPE, 2))
                dve.tensor_tensor(rope_sum[:, :, :], rope_cos[:, :, :], rope_sin[:, :, :], ALU.add
                                  ).then_inc(dve_rope, 1)
                dve.wait_ge(dve_rope, n.count(N_ROPE, 3))
                dve.tensor_copy(rope_hi[:, :, :], rope_sum[:, :, :]).then_inc(dve_rope, 1)
                dve.wait_ge(dve_rope, n.count(N_ROPE, 4))
                wait(dve, st_rope, n.count(32, 0))
                for j, lo_rows in enumerate([lo_rows_q, lo_rows_k]):
                    dve.scalar_tensor_tensor(rope_st[:, j, :], rope_hi[:, j, :], lo_rows[0:ROPE_ROWS, 0:1],
                                             rope_sum[:, j, :], ALU.mult, ALU.add).then_inc(dve_rope, 1)

            def place_values(n):
                dve.wait_ge(pe_v, n.count(1, 1))
                wait(dve, pe_av, n.count(N_AV, -N_AV))
                for t in range(NT):
                    to = v_pad[:, n.parity, t, :, :].rearrange("p h c -> p (h c)")
                    v = xbank[:, t * P:(t + 1) * P]
                    dst = bass.AP(to.tensor, to.offset, [list(to.ap[0]), [96, 4], [41, 3], [1, HD]])
                    dve.tensor_copy(dst, v[:, 0:12 * HD].rearrange("p (j i d) -> p j i d", j=4, i=3)
                                    ).then_inc(dve_v, 1)
                v = xbank[:, 0:NT * P].rearrange("p (t h d) -> p t h d", t=NT, d=HD)
                dve.tensor_copy(v_pad[:, n.parity, :, 12:NH, 0:HD], v[:, :, 12:NH, :]).then_inc(dve_v, 1)

            def normalise(n):
                dve.wait_ge(pe_avT, n.count(1, 1))
                a = xbank[:, 0:NT * P].rearrange("p (t j c) -> p t j c", t=NT, j=4)
                b = xbank[:, NT * P:2 * NT * P].rearrange("p (t j c) -> p t j c", t=NT, j=4)
                dve.reciprocal(sum_inv[:, :, 0:12].rearrange("p t (j i) -> p t j i", j=4),
                               a[:, :, :, SUMCOL:27:9]).then_inc(dve_norm, 1)
                dve.reciprocal(sum_inv[:, :, 12:NH].unsqueeze(3), b[:, :, :, SUMCOL:SUMCOL + 1]).then_inc(dve_norm, 1)
                dve.wait_ge(dve_norm, n.count(N_NORM, 2))
                for t in range(NT):
                    dve.tensor_tensor(
                        attn[:, t, 0:12 * HD].rearrange("p (j i d) -> p j i d", j=4, i=3),
                        a[:, t, :, 0:27].rearrange("p j (i c) -> p j i c", c=9)[:, :, :, 0:HD],
                        sum_inv[:, t, 0:12].rearrange("p (j i) -> p j i", j=4).unsqueeze(3).to_broadcast([P, 4, 3, HD]),
                        ALU.mult).then_inc(dve_norm, 1)
                dve.tensor_tensor(attn[:, :, 12 * HD:D].rearrange("p t (j d) -> p t j d", d=HD), b[:, :, :, 0:HD],
                                  sum_inv[:, :, 12:NH].unsqueeze(3).to_broadcast([P, NT, 4, HD]),
                                  ALU.mult).then_inc(dve_norm, 1)

            def moments(n, of, stats, mv, done, per_batch, first):
                dve.wait_ge(done, n.count(per_batch, first))
                for t in range(NT):
                    dve.bn_stats(stats[:, t, :], of[:, t, :]).then_inc(done, 1)
                wait_before(dve, done, n.count(per_batch, first + NT), dve_passed)
                for t in range(NT):
                    dve.bn_aggr(mv[:, t, :], stats[:, t, :]).then_inc(done, 1)

            def scaled(n, of, mv, rstd, to, made, done):
                dve.wait_ge(made, n.count(2, 2))
                for t in range(NT):
                    dve.tensor_scalar(to[:, n.parity, t, :], of[:, t, :], mv[:, t, 0:1], rstd[:, t:t + 1],
                                      ALU.subtract, ALU.mult).then_inc(done, 1)

            def residual1(n):
                dve.wait_ge(pe_o, n.count(1, 1))
                dve.wait_ge(ld_r[n.parity], n.pair * 16 + 16)
                dve.tensor_tensor(res1[:, :, :].rearrange("p t d -> p (t d)"), xbank[:, 0:T],
                                  xres[:, n.parity, :, :].rearrange("p t d -> p (t d)"), ALU.add).then_inc(dve_ln1, 1)
                moments(n, res1, stats1, mv1, dve_ln1, N_LN, 1)

            def norm1(n):
                scaled(n, res1, mv1, rstd1, x1, pool_rstd1, dve_ln1)

            def split_x1(n):
                dve.wait_ge(act_x1_hi, n.count(1, 1))
                dve.scalar_tensor_tensor(x1_lo[:, n.parity, :], xbank[:, 0:T], X_SCALE, x1_hi[:, n.parity, :],
                                         ALU.mult, ALU.subtract).then_inc(dve_x1_lo, 1)

            def route(n):
                dve.wait_ge(pe_logit, n.count(1, 1))
                dve.tensor_copy(logits[:, :, :].rearrange("p t e -> p (t e)"), xbank[:, 0:NT * NE]
                                ).then_inc(dve_route, 1)
                wait_before(dve, dve_route, n.count(N_ROUTE, 1), dve_passed)
                for t in range(NT):
                    dve.max(top[:, n.parity, t, :], logits[:, t, :]).then_inc(dve_route, 1)
                wait_before(dve, dve_route, n.count(N_ROUTE, 3), dve_passed)
                for t in range(NT):
                    dve.max_index(top_at[:, n.parity, t, :], top[:, n.parity, t, :], logits[:, t, :]
                                  ).then_inc(dve_route, 1)
                dve.tensor_tensor(gap[:, n.parity, :], top[:, n.parity, :, 1], top[:, n.parity, :, 0], ALU.subtract
                                  ).then_inc(dve_route, 1)

            def make_gates(n):
                dve.wait_ge(act_gap, n.count(1, 1))
                dve.tensor_copy(top_no[:, :, :], top_at[:, n.parity, :, :]).then_inc(dve_gate, 1)
                dve.tensor_scalar(gate_den[:, :], gap_exp[:, :], 1.0, None, ALU.add).then_inc(dve_gate, 1)
                dve.wait_ge(dve_gate, n.count(N_GATE, 2))
                dve.reciprocal(gate1[:, :], gate_den[:, :]).then_inc(dve_gate, 1)
                dve.wait_ge(dve_gate, n.count(N_GATE, 3))
                dve.tensor_tensor(gate2[:, :], gap_exp[:, :], gate1[:, :], ALU.mult).then_inc(dve_gate, 1)
                dve.wait_ge(dve_gate, n.count(N_GATE, 4))
                for j, (pick, gate) in enumerate([(pick1, gate1), (pick2, gate2)]):
                    for t in range(NT):
                        dve.tensor_scalar(pick[:, t, :], expert_no[:, :], top_no[:, t, j:j + 1], gate[:, t:t + 1],
                                          ALU.is_equal, ALU.mult).then_inc(dve_gate, 1)
                dve.wait_ge(dve_gate, n.count(N_GATE, 8))
                dve.tensor_tensor(gates[:, n.parity, :, :], pick1[:, :, :], pick2[:, :, :], ALU.add
                                  ).then_inc(dve_gate, 1)

            def reduce_max(n, g):
                dve.wait_ge(pe_max, n.count(N_GROUPS, g + 1))
                if g == 0:
                    wait(dve, pe_nmT, n.count(1, 0))
                t, h0, nh = MAX_GROUPS[g]
                dve.tensor_reduce(neg_max[:, t, h0:h0 + nh], mbank[:, g % 2, :].rearrange("p (h k) -> p h k", h=nh),
                                  AX_X, ALU.max, negate=True).then_inc(dve_max, 1)

            def split_max(n):
                dve.wait_ge(pe_nmT, n.count(1, 1))
                wait(dve, st_max, n.count(32, 0))
                dve.tensor_copy(nm_hi[:, :], xbank[0:NH, 0:T]).then_inc(dve_nm, 1)
                dve.wait_ge(dve_nm, n.count(2, 1))
                dve.tensor_tensor(nm_lo[:, :], xbank[0:NH, 0:T], nm_hi[:, :], ALU.subtract).then_inc(dve_nm, 1)

            def add_expert(n, e):
                dve.wait_ge(pe_down, n.count(NX, e + 1))
                if e == 0:
                    wait(dve, dve_ln2, n.count(N_LN - 1, 0))
                    dve.tensor_tensor(acc[:, :, :].rearrange("p t d -> p (t d)"), ybank[:, 0:T],
                                      x1[:, n.parity, :, :].rearrange("p t d -> p (t d)"), ALU.add
                                      ).then_inc(dve_sum, 1)
                    return
                if e == 1:
                    dve.wait_ge(dve_gate, n.count(N_GATE, N_GATE))
                dve.wait_ge(dve_sum, n.count(N_SUM, 1 + NT * (e - 1)))
                for t in range(NT):
                    dve.scalar_tensor_tensor(acc[:, t, :], ybank[:, t * D:(t + 1) * D],
                                             gates[:, n.parity, t, e - 1:e], acc[:, t, :], ALU.mult, ALU.add
                                             ).then_inc(dve_sum, 1)

            def moments2(n):
                dve.wait_ge(dve_sum, n.count(N_SUM, N_SUM))
                for t in range(NT):
                    dve.bn_stats(stats2[:, t, :], acc[:, t, :]).then_inc(dve_ln2, 1)
                wait_before(dve, dve_ln2, n.count(N_LN - 1, NT), dve_passed)
                for t in range(NT):
                    dve.bn_aggr(mv2[:, t, :], stats2[:, t, :]).then_inc(dve_ln2, 1)

            def norm2(n):
                wait(dve, st_out[n.parity], n.pair * 16)
                scaled(n, acc, mv2, rstd2, yout, pool_rstd2, dve_ln2)

            def iteration(at):
                front, post, ups, downs = at(1), at(-1), at(-2), at(-3)
                e_down = g_max = 0
                for slot in range(SLOTS):
                    if slot == 0 and ups.exists:
                        make_gates(ups)
                    if slot < 6 and downs.exists:
                        add_expert(downs, e_down)
                        e_down += 1
                    if slot == 0 and front.exists:
                        split_qk(front)
                    if slot == 1 and front.exists:
                        rope_products(front, pe_rope, 0, rope_cos, 0)
                    if slot == 2 and front.exists:
                        rope_products(front, pe_swap, 1, rope_sin, 1)
                        rope_stacks(front)
                    if slot == 3 and post.exists:
                        normalise(post)
                    if slot == 4 and front.exists:
                        place_values(front)
                    if slot < 6 and downs.exists:
                        for _ in range(DOWN_IN_SLOT[slot] - 1):
                            add_expert(downs, e_down)
                            e_down += 1
                    if slot == 5 and downs.exists:
                        moments2(downs)
                    if slot == 7 and post.exists:
                        residual1(post)
                    if slot == 7 and downs.exists:
                        norm2(downs)
                    if slot == 9 and post.exists:
                        split_x1(post)
                    if slot == 10 and post.exists:
                        route(post)
                    if 6 <= slot < 11 and front.exists:
                        for _ in range(MAX_IN_SLOT[slot - 6]):
                            reduce_max(front, g_max)
                            g_max += 1
                    if slot == 8 and post.exists:
                        norm1(post)
                    if slot == 11 and front.exists:
                        split_max(front)

            walk(dve, iteration)


_INS = ["L0_attn_x", "L0_attn_W_kv_down", "L0_attn_W_k_up", "L0_attn_W_v_up", "L0_attn_W_q", "L0_attn_W_q_rope",
        "L0_attn_W_k_rope", "L0_attn_W_o", "L0_ffn_Wg", "L0_ffn_Wu", "L0_ffn_Wd", "L0_ffn_W1", "L0_ffn_W2"]


def rope_tables():
    inv_freq = (1.0 / np.float32(10000.0) ** (np.arange(0, DR, 2, dtype=np.float32) / np.float32(DR))).astype(np.float32)
    angle = np.outer(np.arange(T, dtype=np.float32), inv_freq).astype(np.float32).T
    cos = np.concatenate([np.cos(angle), np.cos(angle)])
    sin = np.concatenate([-np.sin(angle), np.sin(angle)])
    both = np.stack([np.tile(cos, (3, 1)), np.tile(sin, (3, 1))], axis=1)
    return np.ascontiguousarray(both.astype(np.float32))


def kernel(**inputs):
    import concourse.bacc as bacc
    from concourse.bass_utils import run_bass_kernel_spmd

    nc = bacc.Bacc("TRN2", target_bir_lowering=False, num_devices=1)
    arrays = {f"in_{name}": np.ascontiguousarray(inputs[name]) for name in _INS}
    arrays["rope_tables"] = rope_tables()
    args = [nc.dram_tensor(name, a.shape, mybir.dt.from_np(a.dtype), kind="ExternalInput").ap()
            for name, a in arrays.items()]
    out = nc.dram_tensor("out", (NB, T, D), F32, kind="ExternalOutput").ap()
    build_layer(nc, *args, out)
    r = run_bass_kernel_spmd(nc, [arrays], core_ids=[0])
    return r.results[0]["out"]
```

```python
from contextlib import ExitStack

import numpy as np

import concourse.bass as bass
from concourse import mybir

ALU = mybir.AluOpType
ACT = mybir.ActivationFunctionType
F32 = mybir.dt.float32
F16 = mybir.dt.float16
BF16 = mybir.dt.bfloat16
U32 = mybir.dt.uint32
AX_X = mybir.AxisListType.X

P = 128
NB, T, D = 32, 256, 128
NT = T // P
NH, HD, DR = 16, 8, 32
NE, F = 8, 256
NF = F // P
NX = NE + 1
EPS = 1e-5
SCORE_SCALE = 1.0 / float(np.sqrt(HD + DR))
X_SCALE, W_SCALE = 16.0, 64.0
UNSCALE = 1.0 / (X_SCALE * W_SCALE)
ROPE_ROWS = 3 * DR
QK_ROWS = ROPE_ROWS + 3 * HD
STACK_ROWS = QK_ROWS + 2
QUADS = [[3 * j + i for j in range(4)] for i in range(3)] + [[12 + j for j in range(4)]]
SUMCOL = HD
HI, LO = 0, 1
N_GROUPS = 12
N_AV = 8
NEG = -1e30
MAX_GROUPS = [(0, 4 * g, 4) for g in range(4)] + [(1, 2 * g, 2) for g in range(8)]
LOOP_FROM, LOOP_TO = 6, 30


PE_ORDER = [
    ("project_rope", 0, 1), ("score_group", 0, 0), ("down", 4, -3), ("score_group", 1, 0),
    ("score_group", 2, 0), ("transpose_av", 0, -1), ("score_group", 3, 0), ("score_group", 4, 0),
    ("score_group", 5, 0), ("score_group", 6, 0), ("project_v", 0, 1), ("down", 5, -3), ("score_group", 7, 0),
    ("score_group", 8, 0), ("transpose_attn", 0, -1), ("score_group", 9, 0), ("values_step", 0, 0),
    ("transpose_x", 0, 2), ("score_group", 10, 0), ("down", 6, -3), ("values_step", 1, 0),
    ("project_out", 0, -1), ("score_group", 11, 0), ("up", 0, -2), ("down_project", 0, 2),
    ("values_step", 2, 0), ("max_group", 0, 1), ("max_group", 1, 1), ("down", 7, -3), ("up", 1, -2),
    ("max_group", 2, 1), ("down", 8, -3), ("max_group", 3, 1), ("up", 2, -2), ("transpose_x1", 0, -1),
    ("max_group", 4, 1), ("up", 3, -2), ("max_group", 5, 1), ("down", 0, -2), ("max_group", 6, 1),
    ("max_group", 7, 1), ("up", 4, -2), ("values_step", 3, 0), ("max_group", 8, 1), ("up", 5, -2),
    ("max_group", 9, 1), ("max_group", 10, 1), ("up", 6, -2), ("max_group", 11, 1), ("router", 0, -1),
    ("down", 1, -2), ("up", 7, -2), ("transpose_max", 0, 1), ("values_step", 4, 0), ("down", 2, -2),
    ("project_qk", 0, 2), ("up", 8, -2), ("values_step", 5, 0), ("down", 3, -2), ("values_step", 6, 0),
    ("values_step", 7, 0),
]
ACT_ORDER = [
    ("exp_group", 1, -2), ("exp_group", 2, -2), ("exp_group", 3, -2), ("exp_group", 4, -2),
    ("exp_group", 5, -2), ("exp_group", 6, -2), ("copy_attnT", 0, -3), ("exp_group", 7, -2),
    ("exp_group", 8, -2), ("copy_xT", 0, 0), ("exp_group", 9, -2), ("exp_group", 10, -2), ("exp_group", 11, -2),
    ("copy_ckv", 0, 0), ("gelu", 0, -4), ("gelu", 1, -4), ("copy_hi_x1", 0, -3), ("gelu", 2, -4),
    ("gelu", 3, -4), ("gelu", 4, -4), ("gelu", 5, -4), ("gap_exponential", 0, -3), ("gelu", 6, -4),
    ("copy_hi_qk", 0, 0), ("gelu", 7, -4), ("gelu", 8, -4), ("copy_av", 0, -2), ("exp_group", 0, -1),
]
DVE_ORDER = [
    ("reduce_max", 0, 0), ("reduce_max", 1, 0), ("add_expert", 7, -4), ("norm1", 0, -2), ("reduce_max", 2, 0),
    ("add_expert", 8, -4), ("reduce_max", 3, 0), ("moments2", 0, -4), ("reduce_max", 4, 0),
    ("reduce_max", 5, 0), ("split_x1", 0, -2), ("reduce_max", 6, 0), ("norm2", 0, -4), ("reduce_max", 7, 0),
    ("reduce_max", 8, 0), ("add_expert", 0, -3), ("reduce_max", 9, 0), ("reduce_max", 10, 0),
    ("reduce_max", 11, 0), ("route", 0, -2), ("add_expert", 1, -3), ("split_max", 0, 0), ("add_expert", 2, -3),
    ("make_gates", 0, -2), ("split_qk", 0, 1), ("add_expert", 3, -3), ("rotate", 0, 1), ("add_expert", 4, -3),
    ("normalise", 0, -1), ("place_values", 0, 1), ("add_expert", 5, -3), ("split_attnT", 0, -1),
    ("split_x", 0, 2), ("add_expert", 6, -3), ("residual1", 0, -1), ("split_ckv", 0, 2),
]
POOL_ORDER = [
    ("mask_group", 2, -1), ("split_hidden", 6, -4), ("split_hidden", 7, -4), ("mask_group", 3, -1),
    ("split_hidden", 8, -4), ("mask_group", 4, -1), ("mask_group", 5, -1), ("mask_group", 6, -1),
    ("mask_group", 7, -1), ("mask_group", 8, -1), ("deviation1", 0, -2), ("split_hidden", 0, -3),
    ("mask_group", 9, -1), ("mask_group", 10, -1), ("deviation2", 0, -4), ("split_hidden", 1, -3),
    ("split_hidden", 2, -3), ("mask_group", 11, -1), ("split_hidden", 3, -3), ("split_hidden", 4, -3),
    ("mask_group", 0, 0), ("split_hidden", 5, -3), ("mask_group", 1, 0),
]
SP_ORDER = [
    ("stack_max", 0, 0), ("load_residual", 0, -1), ("load_x", 0, 2), ("store", 0, -4), ("stack_heads", 0, 1),
    ("stack_rope", 0, 1),
]


class Batch:

    def __init__(self, index, pair, parity):
        self.index, self.pair, self.parity = index, pair, parity
        self.exists = not isinstance(index, int) or 0 <= index < NB

    def count(self, per_batch, j=0):
        return self.index * per_batch + j

    def before(self, k):
        return Batch(self.index - k, None, (self.parity + k) % 2)


def walk(engine, iteration):

    def plain(i):
        def at(offset):
            n = i + offset
            return Batch(n, n // 2, n % 2)
        iteration(at)

    def looped(k, half):
        def at(offset):
            n = half + offset
            return Batch(2 * k + n, k + n // 2, n % 2)
        iteration(at)

    for i in range(-2, LOOP_FROM):
        plain(i)
    with engine.Fori(LOOP_FROM // 2, LOOP_TO // 2) as k:
        looped(k, 0)
        looped(k, 1)
    for i in range(LOOP_TO, NB + 4):
        plain(i)


def run(engine, order, steps):

    def iteration(at):
        for step, j, ahead in order:
            n = at(ahead)
            if n.exists:
                steps[step](n, j)

    walk(engine, iteration)


def wait(engine, semaphore, value):
    if not isinstance(value, int) or value > 0:
        engine.wait_ge(semaphore, value)


def wait_before(engine, semaphore, value, passed):
    engine.wait_ge(semaphore, value)
    engine.sem_inc(passed, 1)


def av_of_group(g):
    return g // 2 if g < 8 else g - 4


def build_layer(nc, x, w_kvd, w_ku, w_vu, w_q, w_qr, w_kr, w_o, w_g, w_u, w_d, w_1, w_2, tables, out):
    ctx = ExitStack()
    with ctx:
        def sb(name, shape, dt=F32):
            return ctx.enter_context(nc.sbuf_tensor(name, shape, dt))

        def ps(name, shape):
            return ctx.enter_context(nc.psum_tensor(name, shape, F32))

        def sem(name):
            return ctx.enter_context(nc.semaphore(name))

        def parts(name, shape):
            return sb(f"{name}_hi", shape, F16), sb(f"{name}_lo", shape, F16)

        wkvd_in = sb("wkvd_in", [P, D])
        wv_in = sb("wv_in", [P, D])
        wo_in = sb("wo_in", [P, D])
        wq_in = sb("wq_in", [P, D])
        wk_in = sb("wk_in", [P, D])
        wqr_in = sb("wqr_in", [P, DR])
        wkr_in = sb("wkr_in", [P, DR])
        wg_in = sb("wg_in", [P, NE])
        wu_in = sb("wu_in", [P, NX, F])
        wd_in = sb("wd_in", [P, NX, NF, D])
        rope = sb("rope", [2 * DR, 2, T])
        wq_dh = sb("wq_dh", [P, HD, NH])
        wk_dh = sb("wk_dh", [P, HD, NH])
        wqr_both = sb("wqr_both", [P, 2, DR])
        wkr_both = sb("wkr_both", [P, 2, DR])
        wkvd, wv, wo = parts("wkvd", [P, D]), parts("wv", [P, D]), parts("wo", [P, D])
        wq, wk = parts("wq", [P, HD, NH]), parts("wk", [P, HD, NH])
        wqr, wkr = parts("wqr", [P, 2, DR]), parts("wkr", [P, 2, DR])
        wg, wu, wd = parts("wg", [P, NE]), parts("wu", [P, NX, F]), parts("wd", [P, NX, NF, D])
        ident = sb("ident", [P, P])
        ident_bf = sb("ident_bf", [P, P], BF16)
        causal = sb("causal", [P, 4, P], BF16)
        minus_half = sb("minus_half", [P, NT])
        expert_no = sb("expert_no", [P, NE])
        expert_int = sb("expert_int", [P, NE], mybir.dt.int32)
        xin = sb("xin", [P, 2, NT, D])
        xT = parts("xT", [P, 2, T])
        ckvT = parts("ckvT", [P, 2, T])
        qk = parts("qk", [P, 2, T])
        rope_cos = sb("rope_cos", [2 * DR, T])
        rope_sin = sb("rope_sin", [2 * DR, T])
        rope_sum = sb("rope_sum", [2 * DR, T])
        rope_hi, rope_lo = parts("roped", [2 * DR, T])
        q_st = sb("q_st", [P, 2, NH, T], F16)
        k_st = sb("k_st", [P, 2, NH, T], F16)
        v_pad = sb("v_pad", [P, 2, NT, NH, 32])
        neg_max = sb("neg_max", [P, NT, NH])
        nm_hi = sb("nm_hi", [NH, T], F16)
        nm_lo = sb("nm_lo", [NH, T], F16)
        probs = sb("probs", [P, N_GROUPS, 512])
        av_sb = sb("av_sb", [P, 2, T])
        sum_inv = sb("sum_inv", [P, NT, NH])
        attn = sb("attn", [P, NT, D])
        attnT = parts("attnT", [P, T])
        xres = sb("xres", [P, 2, NT, D])
        res1 = sb("res1", [P, NT, D])
        stats1 = sb("stats1", [P, NT, 6])
        mv1 = sb("mv1", [P, NT, 2])
        ve1 = sb("ve1", [P, NT])
        rstd1 = sb("rstd1", [P, NT])
        x1 = sb("x1", [P, 2, NT, D])
        x1T = parts("x1T", [P, 2, T])
        top = sb("top", [P, 2, NT, 8])
        top_at = sb("top_at", [P, 2, NT, 8], U32)
        logits = sb("logits", [P, NT, NE])
        gap = sb("gap", [P, 2, NT])
        gap_exp = sb("gap_exp", [P, NT])
        top_no = sb("top_no", [P, NT, 8])
        gate_den = sb("gate_den", [P, NT])
        gate1 = sb("gate1", [P, NT])
        gate2 = sb("gate2", [P, NT])
        pick1 = sb("pick1", [P, NT, NE])
        pick2 = sb("pick2", [P, NT, NE])
        gates = sb("gates", [P, 2, NT, NE])
        hid_full = sb("hid_full", [P, NX, NF * T])
        hid = parts("hid", [P, NX, NF * T])
        acc = sb("acc", [P, NT, D])
        stats2 = sb("stats2", [P, NT, 6])
        mv2 = sb("mv2", [P, NT, 2])
        ve2 = sb("ve2", [P, NT])
        rstd2 = sb("rstd2", [P, NT])
        yout = sb("yout", [P, 2, NT, D])

        ring = ps("ring", [P, 3, 512])
        mbank = ps("mbank", [P, 2, 512])
        avbank = ps("avbank", [P, 2, T])
        xbank = ps("xbank", [P, 512])
        ybank = ps("ybank", [P, 512])

        ld_w = sem("ld_w")
        consts_made = sem("consts_made")
        weights_made = sem("weights_made")
        ld_x = [sem("ld_x0"), sem("ld_x1")]
        ld_r = [sem("ld_r0"), sem("ld_r1")]
        st_qk = sem("st_qk")
        st_rope = sem("st_rope")
        st_max = sem("st_max")
        st_out = [sem("st_out0"), sem("st_out1")]
        pe_xT = sem("pe_xT")
        pe_ckv = sem("pe_ckv")
        pe_qk = sem("pe_qk")
        pe_rope = sem("pe_rope")
        pe_v = sem("pe_v")
        pe_max = sem("pe_max")
        pe_nmT = sem("pe_nmT")
        pe_score = sem("pe_score")
        pe_av = sem("pe_av")
        pe_avT = sem("pe_avT")
        pe_attnT = sem("pe_attnT")
        pe_o = sem("pe_o")
        pe_x1T = sem("pe_x1T")
        pe_logit = sem("pe_logit")
        pe_up = sem("pe_up")
        pe_down = sem("pe_down")
        act_xT = sem("act_xT")
        act_ckv = sem("act_ckv")
        act_qk_hi = sem("act_qk_hi")
        act_exp = sem("act_exp")
        act_av = sem("act_av")
        act_attnT = sem("act_attnT")
        act_x1_hi = sem("act_x1_hi")
        act_gap = sem("act_gap")
        act_gelu = sem("act_gelu")
        pool_mask = sem("pool_mask")
        pool_hid = sem("pool_hid")
        pool_rstd1 = sem("pool_rstd1")
        pool_rstd2 = sem("pool_rstd2")
        pool_passed = sem("pool_passed")
        dve_passed = sem("dve_passed")
        dve_x_lo = sem("dve_x_lo")
        dve_ckv_lo = sem("dve_ckv_lo")
        dve_attnT_lo = sem("dve_attnT_lo")
        dve_qk_lo = sem("dve_qk_lo")
        dve_rope = sem("dve_rope")
        dve_v = sem("dve_v")
        dve_norm = sem("dve_norm")
        dve_ln1 = sem("dve_ln1")
        dve_x1_lo = sem("dve_x1_lo")
        dve_route = sem("dve_route")
        dve_gate = sem("dve_gate")
        dve_max = sem("dve_max")
        dve_nm = sem("dve_nm")
        dve_sum = sem("dve_sum")
        dve_ln2 = sem("dve_ln2")
        CONSTS, WEIGHTS = 8, 28
        N_ROPE, N_V, N_NORM, N_LN, N_ROUTE, N_GATE = 5, 3, 5, 7, 6, 9
        N_SUM = 1 + NE * NT

        x_tiles = x.rearrange("b (t p) d -> b p t d", p=P)
        out_tiles = out.rearrange("b (t p) d -> b p t d", p=P)

        def dram_batch(ap, batch):
            return ap[bass.ds(batch.index, 1)].rearrange("b p t d -> (b p) t d")

        weight_loads = [
            (wkvd_in[:, :], w_kvd), (wq_in[:, :], w_q), (wk_in[:, :], w_ku), (wqr_in[:, :], w_qr),
            (wkr_in[:, :], w_kr), (rope[:, :, :], tables), (wv_in[:, :], w_vu), (wo_in[:, :], w_o),
            (wg_in[:, :], w_g), (wu_in[:, 0, :], w_1),
            (wu_in[:, 1:NX, :], w_u.rearrange("e p f -> p e f")),
            (wd_in[:, 0, :, :], w_2.rearrange("(c p) d -> p c d", p=P)),
            (wd_in[:, 1:NX, :, :], w_d.rearrange("e (c p) d -> p e c d", p=P)),
        ]
        ALL_WEIGHTS = 16 * len(weight_loads)

        block = ctx.enter_context(nc.Block())

        @block.sync
        def _(sp):
            for to, source in weight_loads:
                sp.dma_start(to, source).then_inc(ld_w, 16)

            def load_x(n, _):
                wait(sp, pe_xT, n.count(1, -1))
                sp.dma_start(xin[:, n.parity], dram_batch(x_tiles, n)).then_inc(ld_x[n.parity], 16)

            def load_residual(n, _):
                wait(sp, dve_ln1, n.count(N_LN, 1 - 2 * N_LN))
                sp.dma_start(xres[:, n.parity], dram_batch(x_tiles, n)).then_inc(ld_r[n.parity], 16)

            def stack_heads(n, _):
                wait(sp, pe_score, n.count(N_GROUPS, -N_GROUPS))
                wait(sp, act_qk_hi, n.count(1, 1))
                wait(sp, dve_qk_lo, n.count(1, 1))
                for j, (q_part, k_part) in enumerate([(HI, HI), (HI, LO), (LO, HI)]):
                    rows = slice(ROPE_ROWS + j * HD, ROPE_ROWS + (j + 1) * HD)
                    sp.dma_start(q_st[rows, n.parity], qk[q_part][:, 0, :]).then_inc(st_qk, 16)
                    sp.dma_start(k_st[rows, n.parity], qk[k_part][:, 1, :]).then_inc(st_qk, 16)

            def stack_rope(n, _):
                wait(sp, dve_rope, n.count(N_ROPE, N_ROPE))
                for j, (q_part, k_part) in enumerate([(rope_hi, rope_hi), (rope_hi, rope_lo), (rope_lo, rope_hi)]):
                    for stack, part, at_row in [(q_st, q_part, 0), (k_st, k_part, DR)]:
                        src = part[at_row:at_row + DR, :].unsqueeze(1).to_broadcast([DR, NH, T])
                        sp.dma_start(stack[j * DR:(j + 1) * DR, n.parity], src).then_inc(st_rope, 16)

            def stack_max(n, _):
                wait(sp, dve_nm, n.count(2, 2))
                for j, part in enumerate([nm_hi, nm_lo]):
                    row = slice(QK_ROWS + j, QK_ROWS + j + 1)
                    sp.dma_start(q_st[row, n.parity], part[:, :]).then_inc(st_max, 16)

            def store(n, _):
                wait(sp, dve_ln2, n.count(N_LN - 1, N_LN - 1))
                sp.dma_start(dram_batch(out_tiles, n), yout[:, n.parity]).then_inc(st_out[n.parity], 16)

            sp.wait_ge(consts_made, 2)
            run(sp, SP_ORDER, {
                "load_x": load_x, "load_residual": load_residual, "stack_heads": stack_heads,
                "stack_rope": stack_rope, "store": store, "stack_max": stack_max,
            })
            for parity in range(2):
                sp.wait_ge(st_out[parity], 16 * NB // 2)

        @block.tensor
        def _(pe):
            def transpose_x(n):
                pe.wait_ge(ld_x[n.parity], n.pair * 16 + 16)
                for t in range(NT):
                    mm = pe.transpose(xbank[:, t * P:(t + 1) * P], xin[:, n.parity, t, :], ident[:, :])
                mm.then_inc(pe_xT, 1)

            def three(to, stationary, moving, start=True, stop=True, place=None):
                terms = [(HI, HI), (HI, LO), (LO, HI)]
                for j, (a, b) in enumerate(terms):
                    mm = pe.matmul(to, stationary[a][...], moving[b][...], start=start and j == 0, stop=stop and j == 2,
                                   tile_position=place)
                return mm

            def down_project(n):
                pe.wait_ge(dve_x_lo, n.count(1, 1))
                three(xbank[:, 0:T], wkvd, [part[:, n.parity, :] for part in xT]).then_inc(pe_ckv, 1)

            def project_qk(n):
                pe.wait_ge(dve_ckv_lo, n.count(1, 1))
                three(xbank[:, 0:T], [w[:, :, :].rearrange("p d h -> p (d h)") for w in wq],
                      [part[:, n.parity, :] for part in xT])
                three(xbank[:, T:2 * T], [w[:, :, :].rearrange("p d h -> p (d h)") for w in wk],
                      [part[:, n.parity, :] for part in ckvT]).then_inc(pe_qk, 1)

            def project_rope(n):
                for swapped in range(2):
                    for j, (a, b) in enumerate([(HI, HI), (HI, LO), (LO, HI)]):
                        for strip, (w, of) in enumerate([(wqr, xT), (wkr, ckvT)]):
                            mm = pe.matmul(xbank[DR * strip:DR * (strip + 1), swapped * T:(swapped + 1) * T],
                                           w[a][:, swapped, :], of[b][:, n.parity, :], start=(j == 0),
                                           stop=(j == 2), tile_position=(0, DR * strip), skip_group_check=True)
                mm.then_inc(pe_rope, 1)

            def project_v(n):
                for t in range(NT):
                    mm = three(xbank[:, t * P:(t + 1) * P], [part[:, n.parity, t * P:(t + 1) * P] for part in ckvT], wv)
                mm.then_inc(pe_v, 1)

            def max_group(n, g):
                if g == 0:
                    pe.wait_ge(st_qk, n.count(96, 96))
                    pe.wait_ge(st_rope, n.count(96, 96))
                wait(pe, dve_max, n.count(N_GROUPS, g - 1))
                t, h0, nh = MAX_GROUPS[g]
                keys = (t + 1) * P
                bank = mbank[:, g % 2, :].rearrange("p (h k) -> p h k", h=nh)
                pe.matmul(bank[:, :, t * P:keys], ident_bf[:, :], causal[:, 0:nh, :],
                          start=True, stop=False, skip_group_check=True)
                for a in range(nh):
                    mm = pe.matmul(bank[:, a, :], q_st[0:QK_ROWS, n.parity, h0 + a, t * P:keys],
                                   k_st[0:QK_ROWS, n.parity, h0 + a, 0:keys],
                                   start=False, stop=(a == nh - 1), skip_group_check=True)
                mm.then_inc(pe_max, 1)

            def transpose_max(n):
                pe.wait_ge(dve_max, n.count(N_GROUPS, N_GROUPS))
                for t in range(NT):
                    mm = pe.transpose(xbank[0:NH, t * P:(t + 1) * P], neg_max[:, t, :], ident[:, :])
                mm.then_inc(pe_nmT, 1)

            def score_group(n, g):
                if g == 0:
                    pe.wait_ge(st_max, n.count(32, 32))
                    pe.wait_ge(dve_v, n.count(N_V, N_V))
                if g >= 3:
                    pe.wait_ge(act_exp, n.count(N_GROUPS, g - 2))
                elif n.before(3).exists:
                    pe.wait_ge(act_gelu, n.before(3).count(NX, NX - 2 + g))
                else:
                    wait(pe, act_exp, n.count(N_GROUPS, g - 2))
                if g < 8:
                    heads, kt = QUADS[g // 2][2 * (g % 2):2 * (g % 2) + 2], 0
                else:
                    heads, kt = QUADS[g - 8], 1
                width = T - kt * P
                for a, h in enumerate(heads):
                    mm = pe.matmul(ring[:, g % 3, a * width:(a + 1) * width],
                                   k_st[0:STACK_ROWS, n.parity, h, kt * P:(kt + 1) * P],
                                   q_st[0:STACK_ROWS, n.parity, h, kt * P:T], start=True, stop=True)
                mm.then_inc(pe_score, 1)

            def values_step(n, s):
                groups = [2 * s, 2 * s + 1] if s < 4 else [s + 4]
                pe.wait_ge(pool_mask, n.count(N_GROUPS, groups[-1] + 1))
                if s == 0:
                    wait(pe, act_av, n.count(1, 0))
                kt, quad = s // 4, s % 4
                part, cols = quad // 3, slice(kt * P, T)
                for j, h in enumerate(QUADS[quad]):
                    if kt == 0:
                        p_cols = probs[:, groups[j // 2], (j % 2) * T:(j % 2 + 1) * T]
                    else:
                        p_cols = probs[:, groups[0], j * P:(j + 1) * P]
                    mm = pe.matmul(avbank[32 * j:32 * j + 32, part, cols], v_pad[:, n.parity, kt, h, :], p_cols,
                                   start=(s == 0), stop=(s == N_AV - 1), skip_group_check=True,
                                   tile_position=(0, 32 * j))
                mm.then_inc(pe_av, 1)

            def transpose_av(n):
                pe.wait_ge(act_av, n.count(1, 1))
                for part in range(2):
                    for t in range(NT):
                        mm = pe.transpose(xbank[:, (part * NT + t) * P:(part * NT + t + 1) * P],
                                          av_sb[:, part, t * P:(t + 1) * P], ident[:, :])
                mm.then_inc(pe_avT, 1)

            def transpose_attn(n):
                pe.wait_ge(dve_norm, n.count(N_NORM, N_NORM))
                for t in range(NT):
                    mm = pe.transpose(xbank[:, t * P:(t + 1) * P], attn[:, t, :], ident[:, :])
                mm.then_inc(pe_attnT, 1)

            def project_out(n):
                pe.wait_ge(dve_attnT_lo, n.count(1, 1))
                for t in range(NT):
                    mm = three(xbank[:, t * P:(t + 1) * P], [part[:, t * P:(t + 1) * P] for part in attnT], wo)
                mm.then_inc(pe_o, 1)

            def transpose_x1(n):
                pe.wait_ge(dve_ln1, n.count(N_LN, N_LN))
                for t in range(NT):
                    mm = pe.transpose(xbank[:, t * P:(t + 1) * P], x1[:, n.parity, t, :], ident[:, :])
                mm.then_inc(pe_x1T, 1)

            def router(n):
                pe.wait_ge(dve_x1_lo, n.count(1, 1))
                for t in range(NT):
                    mm = three(xbank[:, t * NE:(t + 1) * NE], [part[:, n.parity, t * P:(t + 1) * P] for part in x1T], wg)
                mm.then_inc(pe_logit, 1)

            def up(n, e):
                if e >= 3:
                    pe.wait_ge(act_gelu, n.count(NX, e - 2))
                elif n.before(-2).exists:
                    pe.wait_ge(act_exp, n.before(-2).count(N_GROUPS, N_GROUPS - 2 + e))
                else:
                    wait(pe, act_gelu, n.count(NX, e - 2))
                for c in range(NF):
                    mm = three(ring[:, e % 3, c * T:(c + 1) * T], [w[:, e, c * P:(c + 1) * P] for w in wu],
                               [part[:, n.parity, :] for part in x1T])
                mm.then_inc(pe_up, 1)

            def down(n, e):
                pe.wait_ge(pool_hid, n.count(NX, e + 1))
                if e == 0:
                    wait(pe, dve_sum, n.count(N_SUM, 0))
                else:
                    pe.wait_ge(dve_sum, n.count(N_SUM, 1 + NT * (e - 1)))
                for t in range(NT):
                    for c in range(NF):
                        at_token = c * T + t * P
                        mm = three(ybank[:, t * D:(t + 1) * D], [part[:, e, at_token:at_token + P] for part in hid],
                                   [w[:, e, c, :] for w in wd], start=(c == 0), stop=(c == NF - 1))
                mm.then_inc(pe_down, 1)

            readers = {
                "transpose_x": (dve_x_lo, 1, 1), "down_project": (dve_ckv_lo, 1, 1), "project_qk": (dve_qk_lo, 1, 1),
                "project_rope": (dve_rope, N_ROPE, 2),
                "project_v": (dve_v, N_V, N_V), "transpose_av": (dve_norm, N_NORM, N_NORM),
                "transpose_attn": (dve_attnT_lo, 1, 1), "project_out": (dve_ln1, N_LN, 1),
                "transpose_x1": (dve_x1_lo, 1, 1), "router": (dve_route, N_ROUTE, 1), "transpose_max": (dve_nm, 2, 2),
            }
            sharing = [(step, ahead) for step, _, ahead in PE_ORDER if step in readers]

            def small(step, product):
                at_place = [other for other, _ in sharing].index(step)

                def taken(n, j):
                    for back in range(1, 4 * len(sharing)):
                        other, ahead = sharing[(at_place - back) % len(sharing)]
                        laps = (back - at_place + len(sharing) - 1) // len(sharing)
                        before = n.before(sharing[at_place][1] - ahead + laps)
                        if before.exists:
                            semaphore, per_batch, count = readers[other]
                            wait(pe, semaphore, before.count(per_batch, count))
                            break
                    product(n)
                return taken

            pe.wait_ge(consts_made, CONSTS)
            pe.wait_ge(weights_made, WEIGHTS)
            pe.wait_ge(ld_w, ALL_WEIGHTS)
            run(pe, PE_ORDER, {
                "transpose_x": small("transpose_x", transpose_x),
                "down_project": small("down_project", down_project),
                "project_qk": small("project_qk", project_qk),
                "project_rope": small("project_rope", project_rope),
                "project_v": small("project_v", project_v),
                "transpose_av": small("transpose_av", transpose_av),
                "transpose_attn": small("transpose_attn", transpose_attn),
                "project_out": small("project_out", project_out),
                "transpose_x1": small("transpose_x1", transpose_x1),
                "router": small("router", router),
                "transpose_max": small("transpose_max", transpose_max),
                "max_group": max_group, "score_group": score_group, "values_step": values_step,
                "up": up, "down": down,
            })

        @block.scalar
        def _(act):
            def copy_hi_qk(n, _):
                pe_done = n.count(1, 1)
                act.wait_ge(pe_qk, pe_done)
                wait(act, st_qk, n.count(96, 0))
                act.mul(qk[HI][:, :, :].rearrange("p a t -> p (a t)"), xbank[:, :], 1.0 / W_SCALE
                        ).then_inc(act_qk_hi, 1)

            def gap_exponential(n, _):
                act.wait_ge(dve_route, n.count(N_ROUTE, N_ROUTE))
                wait(act, dve_gate, n.count(N_GATE, 0))
                act.activation(gap_exp[:, :], gap[:, n.parity, :], ACT.Exp, scale=UNSCALE).then_inc(act_gap, 1)

            def exp_group(n, g):
                act.wait_ge(pe_score, n.count(N_GROUPS, g + 1))
                wait(act, pe_av, n.count(N_AV, av_of_group(g) + 1 - N_AV))
                act.activation(probs[:, g, :], ring[:, g % 3, :], ACT.Exp, scale=SCORE_SCALE
                               ).then_inc(act_exp, 1)

            def copy_av(n, _):
                act.wait_ge(pe_av, n.count(N_AV, N_AV))
                wait(act, pe_avT, n.count(1, 0))
                act.copy(av_sb[:, :, :], avbank[:, :, :]).then_inc(act_av, 1)

            def copy_attnT(n, _):
                act.wait_ge(pe_attnT, n.count(1, 1))
                wait(act, pe_o, n.count(1, 0))
                act.copy(attnT[HI][:, :], xbank[:, 0:T]).then_inc(act_attnT, 1)

            def copy_xT(n, _):
                act.wait_ge(pe_xT, n.count(1, 1))
                wait(act, pe_qk, n.count(1, -1))
                wait(act, pe_rope, n.count(1, -1))
                act.copy(xT[HI][:, n.parity, :], xbank[:, 0:T]).then_inc(act_xT, 1)

            def copy_ckv(n, _):
                act.wait_ge(pe_ckv, n.count(1, 1))
                wait(act, pe_qk, n.count(1, -1))
                wait(act, pe_rope, n.count(1, -1))
                wait(act, pe_v, n.count(1, -1))
                act.mul(ckvT[HI][:, n.parity, :], xbank[:, 0:T], 1.0 / W_SCALE).then_inc(act_ckv, 1)

            def copy_hi_x1(n, _):
                act.wait_ge(pe_x1T, n.count(1, 1))
                wait(act, pe_up, n.count(NX, -NX))
                act.mul(x1T[HI][:, n.parity, :], xbank[:, 0:T], X_SCALE).then_inc(act_x1_hi, 1)

            def gelu(n, e):
                act.wait_ge(pe_up, n.count(NX, e + 1))
                wait(act, pe_down, n.count(NX, e + 1 - NX))
                act.activation(hid[HI][:, e, :], ring[:, e % 3, :], ACT.Gelu, scale=UNSCALE)
                wait(act, pool_hid, n.count(NX, e + 1 - NX))
                act.activation(hid_full[:, e, :], ring[:, e % 3, :], ACT.Gelu, scale=UNSCALE
                               ).then_inc(act_gelu, 1)

            run(act, ACT_ORDER, {
                "copy_xT": copy_xT, "copy_ckv": copy_ckv, "copy_hi_qk": copy_hi_qk, "exp_group": exp_group,
                "copy_av": copy_av, "copy_attnT": copy_attnT, "copy_hi_x1": copy_hi_x1,
                "gap_exponential": gap_exponential, "gelu": gelu,
            })

        @block.gpsimd
        def _(pool):
            pool.memset(q_st[:, :, :, :], 0.0).then_inc(consts_made, 1)
            pool.wait_ge(consts_made, 1)
            pool.memset(k_st[96:P, :, :, :], 1.0).then_inc(consts_made, 1)
            pool.wait_ge(consts_made, 2)
            pool.memset(ident[:, :], 0.0).then_inc(consts_made, 1)
            pool.wait_ge(consts_made, 3)
            pool.affine_select(out=ident[:, :], in_=ident[:, :], compare_op=ALU.not_equal, fill=1.0, base=0,
                               pattern=[[-1, P]], channel_multiplier=1).then_inc(consts_made, 1)
            pool.wait_ge(consts_made, 4)
            pool.memset(causal[:, :, :], 0.0).then_inc(consts_made, 1)
            pool.wait_ge(consts_made, 5)
            pool.affine_select(out=causal[:, :, :], in_=causal[:, :, :], compare_op=ALU.is_ge, fill=NEG, base=0,
                               pattern=[[0, 4], [-1, P]], channel_multiplier=1).then_inc(consts_made, 1)
            pool.wait_ge(consts_made, 6)
            pool.memset(minus_half[:, :], -0.5).then_inc(consts_made, 1)
            pool.wait_ge(consts_made, 7)
            pool.iota(expert_int[:, :], pattern=[[1, NE]], base=0, channel_multiplier=0).then_inc(consts_made, 1)
            pool.wait_ge(consts_made, CONSTS)

            def mask_group(n, g):
                wait_before(pool, act_exp, n.count(N_GROUPS, g + 1), pool_passed)
                heads = 2 if g < 8 else 4
                block_of = probs[:, g, :].rearrange("p (a q) -> p a q", a=heads)[:, :, 0:P]
                pool.affine_select(out=block_of, in_=block_of, compare_op=ALU.is_ge, fill=0.0, base=0,
                                   pattern=[[0, heads], [1, P]], channel_multiplier=-1).then_inc(pool_mask, 1)

            def split_hidden(n, e):
                pool.wait_ge(act_gelu, n.count(NX, e + 1))
                wait(pool, pe_down, n.count(NX, e + 1 - NX))
                pool.tensor_tensor(hid[LO][:, e, :], hid_full[:, e, :], hid[HI][:, e, :], ALU.subtract
                                   ).then_inc(pool_hid, 1)

            def inverse_deviation(n, made, mv, ve, rstd, done):
                wait_before(pool, made[0], made[1], pool_passed)
                pool.tensor_scalar(ve[:, :], mv[:, :, 1], EPS, None, ALU.add).then_inc(done, 1)
                pool.wait_ge(done, n.count(2, 1))
                pool.tensor_tensor(rstd[:, :], ve[:, :], minus_half[:, :], ALU.pow).then_inc(done, 1)

            def deviation1(n, _):
                inverse_deviation(n, (dve_ln1, n.count(N_LN, 5)), mv1, ve1, rstd1, pool_rstd1)

            def deviation2(n, _):
                inverse_deviation(n, (dve_ln2, n.count(N_LN - 1, 4)), mv2, ve2, rstd2, pool_rstd2)

            run(pool, POOL_ORDER, {"mask_group": mask_group, "split_hidden": split_hidden, "deviation1": deviation1, "deviation2": deviation2})

        @block.vector
        def _(dve):
            dve.memset(v_pad[:, :, :, :, :], 0.0).then_inc(weights_made, 1)
            dve.wait_ge(weights_made, 1)
            for parity in range(2):
                for t in range(NT):
                    for quad, heads in enumerate(QUADS):
                        at_col = 9 * quad + SUMCOL if quad < 3 else SUMCOL
                        step = heads[1] - heads[0]
                        ones = dve.memset(v_pad[:, parity, t, heads[0]:heads[3] + 1:step, at_col:at_col + 1], 1.0)
            ones.then_inc(weights_made, 1)
            dve.wait_ge(ld_w, ALL_WEIGHTS)
            for w_in, w_to in [(wq_in, wq_dh), (wk_in, wk_dh)]:
                dve.tensor_copy(w_to[:, :, :], w_in[:, :].rearrange("p (h d) -> p d h", d=HD)
                                ).then_inc(weights_made, 1)
            half = DR // 2
            for w_in, w_both in [(wqr_in, wqr_both), (wkr_in, wkr_both)]:
                dve.tensor_copy(w_both[:, 0, :], w_in[:, :])
                dve.tensor_copy(w_both[:, 1, 0:half], w_in[:, half:DR])
                dve.tensor_copy(w_both[:, 1, half:DR], w_in[:, 0:half]).then_inc(weights_made, 1)
            splits = [(wkvd_in, wkvd), (wv_in, wv), (wo_in, wo), (wg_in, wg), (wu_in, wu), (wd_in, wd),
                      (wq_dh, wq), (wk_dh, wk), (wqr_both, wqr), (wkr_both, wkr)]
            dve.wait_ge(weights_made, 6)
            for w_in, (hi, lo) in splits:
                dve.tensor_scalar(hi[...], w_in[...], W_SCALE, None, ALU.mult).then_inc(weights_made, 1)
            dve.wait_ge(weights_made, 6 + len(splits))
            for w_in, (hi, lo) in splits:
                dve.scalar_tensor_tensor(lo[...], w_in[...], W_SCALE, hi[...], ALU.mult, ALU.subtract
                                         ).then_inc(weights_made, 1)
            dve.wait_ge(consts_made, CONSTS)
            dve.tensor_copy(ident_bf[:, :], ident[:, :]).then_inc(weights_made, 1)
            dve.tensor_copy(expert_no[:, :], expert_int[:, :]).then_inc(weights_made, 1)
            dve.wait_ge(weights_made, WEIGHTS)

            def low_part(lo, hi, of, scale, done):
                dve.scalar_tensor_tensor(lo, of, scale, hi, ALU.mult, ALU.subtract).then_inc(done, 1)

            def split_x(n, _):
                dve.wait_ge(act_xT, n.count(1, 1))
                low_part(xT[LO][:, n.parity, :], xT[HI][:, n.parity, :], xbank[:, 0:T], 1.0, dve_x_lo)

            def split_ckv(n, _):
                dve.wait_ge(act_ckv, n.count(1, 1))
                low_part(ckvT[LO][:, n.parity, :], ckvT[HI][:, n.parity, :], xbank[:, 0:T], 1.0 / W_SCALE, dve_ckv_lo)

            def split_attnT(n, _):
                dve.wait_ge(act_attnT, n.count(1, 1))
                low_part(attnT[LO][:, :], attnT[HI][:, :], xbank[:, 0:T], 1.0, dve_attnT_lo)

            def split_qk(n, _):
                dve.wait_ge(act_qk_hi, n.count(1, 1))
                wait(dve, st_qk, n.count(96, 0))
                low_part(qk[LO][:, :, :].rearrange("p a t -> p (a t)"), qk[HI][:, :, :].rearrange("p a t -> p (a t)"),
                         xbank[:, :], 1.0 / W_SCALE, dve_qk_lo)

            def rotate(n, _):
                dve.wait_ge(pe_rope, n.count(1, 1))
                rows = slice(0, 2 * DR)
                dve.tensor_tensor(rope_cos[:, :], xbank[rows, 0:T], rope[:, 0, :], ALU.mult).then_inc(dve_rope, 1)
                dve.tensor_tensor(rope_sin[:, :], xbank[rows, T:2 * T], rope[:, 1, :], ALU.mult).then_inc(dve_rope, 1)
                dve.wait_ge(dve_rope, n.count(N_ROPE, 2))
                dve.tensor_tensor(rope_sum[:, :], rope_cos[:, :], rope_sin[:, :], ALU.add).then_inc(dve_rope, 1)
                dve.wait_ge(dve_rope, n.count(N_ROPE, 3))
                wait(dve, st_rope, n.count(96, 0))
                dve.tensor_copy(rope_hi[:, :], rope_sum[:, :]).then_inc(dve_rope, 1)
                dve.wait_ge(dve_rope, n.count(N_ROPE, 4))
                low_part(rope_lo[:, :], rope_hi[:, :], rope_sum[:, :], 1.0, dve_rope)

            def place_values(n, _):
                dve.wait_ge(pe_v, n.count(1, 1))
                wait(dve, pe_av, n.count(N_AV, -N_AV))
                for t in range(NT):
                    to = v_pad[:, n.parity, t, :, :].rearrange("p h c -> p (h c)")
                    v = xbank[:, t * P:(t + 1) * P]
                    dst = bass.AP(to.tensor, to.offset, [list(to.ap[0]), [96, 4], [41, 3], [1, HD]])
                    dve.tensor_scalar(dst, v[:, 0:12 * HD].rearrange("p (j i d) -> p j i d", j=4, i=3),
                                      1.0 / W_SCALE, None, ALU.mult).then_inc(dve_v, 1)
                v = xbank[:, 0:NT * P].rearrange("p (t h d) -> p t h d", t=NT, d=HD)
                dve.tensor_scalar(v_pad[:, n.parity, :, 12:NH, 0:HD], v[:, :, 12:NH, :], 1.0 / W_SCALE, None,
                                  ALU.mult).then_inc(dve_v, 1)

            def normalise(n, _):
                dve.wait_ge(pe_avT, n.count(1, 1))
                a = xbank[:, 0:NT * P].rearrange("p (t j c) -> p t j c", t=NT, j=4)
                b = xbank[:, NT * P:2 * NT * P].rearrange("p (t j c) -> p t j c", t=NT, j=4)
                dve.reciprocal(sum_inv[:, :, 0:12].rearrange("p t (j i) -> p t j i", j=4),
                               a[:, :, :, SUMCOL:27:9]).then_inc(dve_norm, 1)
                dve.reciprocal(sum_inv[:, :, 12:NH].unsqueeze(3), b[:, :, :, SUMCOL:SUMCOL + 1]).then_inc(dve_norm, 1)
                dve.wait_ge(dve_norm, n.count(N_NORM, 2))
                for t in range(NT):
                    dve.tensor_tensor(
                        attn[:, t, 0:12 * HD].rearrange("p (j i d) -> p j i d", j=4, i=3),
                        a[:, t, :, 0:27].rearrange("p j (i c) -> p j i c", c=9)[:, :, :, 0:HD],
                        sum_inv[:, t, 0:12].rearrange("p (j i) -> p j i", j=4).unsqueeze(3).to_broadcast([P, 4, 3, HD]),
                        ALU.mult).then_inc(dve_norm, 1)
                dve.tensor_tensor(attn[:, :, 12 * HD:D].rearrange("p t (j d) -> p t j d", d=HD), b[:, :, :, 0:HD],
                                  sum_inv[:, :, 12:NH].unsqueeze(3).to_broadcast([P, NT, 4, HD]),
                                  ALU.mult).then_inc(dve_norm, 1)

            def moments(n, of, stats, mv, done, per_batch, first):
                dve.wait_ge(done, n.count(per_batch, first))
                for t in range(NT):
                    dve.bn_stats(stats[:, t, :], of[:, t, :]).then_inc(done, 1)
                wait_before(dve, done, n.count(per_batch, first + NT), dve_passed)
                for t in range(NT):
                    dve.bn_aggr(mv[:, t, :], stats[:, t, :]).then_inc(done, 1)

            def scaled(n, of, mv, rstd, to, made, done):
                dve.wait_ge(made, n.count(2, 2))
                for t in range(NT):
                    dve.tensor_scalar(to[:, n.parity, t, :], of[:, t, :], mv[:, t, 0:1], rstd[:, t:t + 1],
                                      ALU.subtract, ALU.mult).then_inc(done, 1)

            def residual1(n, _):
                dve.wait_ge(pe_o, n.count(1, 1))
                dve.wait_ge(ld_r[n.parity], n.pair * 16 + 16)
                dve.scalar_tensor_tensor(res1[:, :, :].rearrange("p t d -> p (t d)"), xbank[:, 0:T], 1.0 / W_SCALE,
                                         xres[:, n.parity, :, :].rearrange("p t d -> p (t d)"),
                                         ALU.mult, ALU.add).then_inc(dve_ln1, 1)
                moments(n, res1, stats1, mv1, dve_ln1, N_LN, 1)

            def norm1(n, _):
                scaled(n, res1, mv1, rstd1, x1, pool_rstd1, dve_ln1)

            def split_x1(n, _):
                dve.wait_ge(act_x1_hi, n.count(1, 1))
                low_part(x1T[LO][:, n.parity, :], x1T[HI][:, n.parity, :], xbank[:, 0:T], X_SCALE, dve_x1_lo)

            def route(n, _):
                dve.wait_ge(pe_logit, n.count(1, 1))
                dve.tensor_copy(logits[:, :, :].rearrange("p t e -> p (t e)"), xbank[:, 0:NT * NE]
                                ).then_inc(dve_route, 1)
                wait_before(dve, dve_route, n.count(N_ROUTE, 1), dve_passed)
                for t in range(NT):
                    dve.max(top[:, n.parity, t, :], logits[:, t, :]).then_inc(dve_route, 1)
                wait_before(dve, dve_route, n.count(N_ROUTE, 3), dve_passed)
                for t in range(NT):
                    dve.max_index(top_at[:, n.parity, t, :], top[:, n.parity, t, :], logits[:, t, :]
                                  ).then_inc(dve_route, 1)
                dve.tensor_tensor(gap[:, n.parity, :], top[:, n.parity, :, 1], top[:, n.parity, :, 0], ALU.subtract
                                  ).then_inc(dve_route, 1)

            def make_gates(n, _):
                dve.wait_ge(act_gap, n.count(1, 1))
                dve.tensor_copy(top_no[:, :, :], top_at[:, n.parity, :, :]).then_inc(dve_gate, 1)
                dve.tensor_scalar(gate_den[:, :], gap_exp[:, :], 1.0, W_SCALE, ALU.add, ALU.mult).then_inc(dve_gate, 1)
                dve.wait_ge(dve_gate, n.count(N_GATE, 2))
                dve.reciprocal(gate1[:, :], gate_den[:, :]).then_inc(dve_gate, 1)
                dve.wait_ge(dve_gate, n.count(N_GATE, 3))
                dve.tensor_tensor(gate2[:, :], gap_exp[:, :], gate1[:, :], ALU.mult).then_inc(dve_gate, 1)
                dve.wait_ge(dve_gate, n.count(N_GATE, 4))
                for j, (pick, gate) in enumerate([(pick1, gate1), (pick2, gate2)]):
                    for t in range(NT):
                        dve.tensor_scalar(pick[:, t, :], expert_no[:, :], top_no[:, t, j:j + 1], gate[:, t:t + 1],
                                          ALU.is_equal, ALU.mult).then_inc(dve_gate, 1)
                dve.wait_ge(dve_gate, n.count(N_GATE, 8))
                dve.tensor_tensor(gates[:, n.parity, :, :], pick1[:, :, :], pick2[:, :, :], ALU.add
                                  ).then_inc(dve_gate, 1)

            def reduce_max(n, g):
                dve.wait_ge(pe_max, n.count(N_GROUPS, g + 1))
                if g == 0:
                    wait(dve, pe_nmT, n.count(1, 0))
                t, h0, nh = MAX_GROUPS[g]
                dve.tensor_reduce(neg_max[:, t, h0:h0 + nh], mbank[:, g % 2, :].rearrange("p (h k) -> p h k", h=nh),
                                  AX_X, ALU.max, negate=True).then_inc(dve_max, 1)

            def split_max(n, _):
                dve.wait_ge(pe_nmT, n.count(1, 1))
                wait(dve, st_max, n.count(32, 0))
                dve.tensor_copy(nm_hi[:, :], xbank[0:NH, 0:T]).then_inc(dve_nm, 1)
                dve.wait_ge(dve_nm, n.count(2, 1))
                dve.tensor_tensor(nm_lo[:, :], xbank[0:NH, 0:T], nm_hi[:, :], ALU.subtract).then_inc(dve_nm, 1)

            def add_expert(n, e):
                dve.wait_ge(pe_down, n.count(NX, e + 1))
                if e == 0:
                    wait(dve, dve_ln2, n.count(N_LN - 1, 0))
                    dve.scalar_tensor_tensor(acc[:, :, :].rearrange("p t d -> p (t d)"), ybank[:, 0:T], 1.0 / W_SCALE,
                                             x1[:, n.parity, :, :].rearrange("p t d -> p (t d)"),
                                             ALU.mult, ALU.add).then_inc(dve_sum, 1)
                    return
                if e == 1:
                    dve.wait_ge(dve_gate, n.count(N_GATE, N_GATE))
                dve.wait_ge(dve_sum, n.count(N_SUM, 1 + NT * (e - 1)))
                for t in range(NT):
                    dve.scalar_tensor_tensor(acc[:, t, :], ybank[:, t * D:(t + 1) * D],
                                             gates[:, n.parity, t, e - 1:e], acc[:, t, :], ALU.mult, ALU.add
                                             ).then_inc(dve_sum, 1)

            def moments2(n, _):
                dve.wait_ge(dve_sum, n.count(N_SUM, N_SUM))
                for t in range(NT):
                    dve.bn_stats(stats2[:, t, :], acc[:, t, :]).then_inc(dve_ln2, 1)
                wait_before(dve, dve_ln2, n.count(N_LN - 1, NT), dve_passed)
                for t in range(NT):
                    dve.bn_aggr(mv2[:, t, :], stats2[:, t, :]).then_inc(dve_ln2, 1)

            def norm2(n, _):
                wait(dve, st_out[n.parity], n.pair * 16)
                scaled(n, acc, mv2, rstd2, yout, pool_rstd2, dve_ln2)

            run(dve, DVE_ORDER, {
                "split_x": split_x, "split_ckv": split_ckv, "split_attnT": split_attnT,
                "split_qk": split_qk, "rotate": rotate, "place_values": place_values, "reduce_max": reduce_max,
                "split_max": split_max, "normalise": normalise, "residual1": residual1, "norm1": norm1,
                "split_x1": split_x1, "route": route, "make_gates": make_gates, "add_expert": add_expert,
                "moments2": moments2, "norm2": norm2,
            })


_INS = ["L0_attn_x", "L0_attn_W_kv_down", "L0_attn_W_k_up", "L0_attn_W_v_up", "L0_attn_W_q", "L0_attn_W_q_rope",
        "L0_attn_W_k_rope", "L0_attn_W_o", "L0_ffn_Wg", "L0_ffn_Wu", "L0_ffn_Wd", "L0_ffn_W1", "L0_ffn_W2"]


def rope_tables():
    inv_freq = (1.0 / np.float32(10000.0) ** (np.arange(0, DR, 2, dtype=np.float32) / np.float32(DR))).astype(np.float32)
    angle = np.outer(np.arange(T, dtype=np.float32), inv_freq).astype(np.float32).T
    cos = np.concatenate([np.cos(angle), np.cos(angle)])
    sin = np.concatenate([-np.sin(angle), np.sin(angle)])
    both = np.stack([np.tile(cos, (2, 1)), np.tile(sin, (2, 1))], axis=1) / W_SCALE
    return np.ascontiguousarray(both.astype(np.float32))


def kernel(**inputs):
    import concourse.bacc as bacc
    from concourse.bass_utils import run_bass_kernel_spmd

    nc = bacc.Bacc("TRN2", target_bir_lowering=False, num_devices=1)
    arrays = {f"in_{name}": np.ascontiguousarray(inputs[name]) for name in _INS}
    arrays["rope_tables"] = rope_tables()
    args = [nc.dram_tensor(name, a.shape, mybir.dt.from_np(a.dtype), kind="ExternalInput").ap()
            for name, a in arrays.items()]
    out = nc.dram_tensor("out", (NB, T, D), F32, kind="ExternalOutput").ap()
    build_layer(nc, *args, out)
    r = run_bass_kernel_spmd(nc, [arrays], core_ids=[0])
    return r.results[0]["out"]
```

```python
from contextlib import ExitStack

import numpy as np

import concourse.bass as bass
from concourse import mybir

ALU = mybir.AluOpType
ACT = mybir.ActivationFunctionType
F32 = mybir.dt.float32
F16 = mybir.dt.float16
BF16 = mybir.dt.bfloat16
U32 = mybir.dt.uint32
AX_X = mybir.AxisListType.X

P = 128
NB, T, D = 32, 256, 128
NT = T // P
NH, HD, DR = 16, 8, 32
NE, F = 8, 256
NF = F // P
NX = NE + 1
EPS = 1e-5
SCORE_SCALE = 1.0 / float(np.sqrt(HD + DR))
X_SCALE, W_SCALE = 16.0, 64.0
UNSCALE = 1.0 / (X_SCALE * W_SCALE)
ROPE_ROWS = 3 * DR
QK_ROWS = ROPE_ROWS + 3 * HD
BLOCK = 32
MASK_ROWS = T // BLOCK - NT
MAX_ROWS = QK_ROWS + MASK_ROWS
STACK_ROWS = MAX_ROWS + 2
QUADS = [[3 * j + i for j in range(4)] for i in range(3)] + [[12 + j for j in range(4)]]
SUMCOL = HD
HI, LO = 0, 1
ATTN_WIDTHS = [D, D, D, 2 * DR, 2 * DR, D, D, NE]
ATTN_AT = [sum(ATTN_WIDTHS[:i]) for i in range(len(ATTN_WIDTHS))]
ATTN_COLS = sum(ATTN_WIDTHS)
N_GROUPS = 12
N_AV = 8
NEG = -1e30
MAX_GROUPS = [(0, 4 * g, 4) for g in range(4)] + [(1, 2 * g, 2) for g in range(8)]
LOOP_FROM, LOOP_TO = 6, 30


PE_ORDER = [
    ("values_step", 4, -1), ("down", 2, -3), ("values_step", 5, -1), ("project_rope", 0, 1),
    ("values_step", 6, -1), ("values_step", 7, -1), ("down", 3, -3), ("score_group", 0, 0),
    ("score_group", 1, 0), ("transpose_av", 0, -1), ("score_group", 2, 0), ("down", 4, -3),
    ("score_group", 3, 0), ("score_group", 4, 0), ("score_group", 5, 0), ("project_v", 0, 1), ("down", 5, -3),
    ("score_group", 6, 0), ("score_group", 7, 0), ("score_group", 8, 0), ("transpose_attn", 0, -1),
    ("values_step", 0, 0), ("score_group", 9, 0), ("down", 6, -3), ("score_group", 10, 0),
    ("score_group", 11, 0), ("project_out", 0, -1), ("up", 0, -2), ("down", 7, -3), ("down_project", 0, 2),
    ("values_step", 1, 0), ("up", 1, -2), ("max_group", 0, 1), ("max_group", 1, 1), ("down", 8, -3),
    ("max_group", 2, 1), ("up", 2, -2), ("up", 3, -2), ("max_group", 3, 1), ("max_group", 4, 1),
    ("down", 0, -2), ("max_group", 5, 1), ("transpose_x1", 0, -1), ("max_group", 6, 1), ("up", 4, -2),
    ("max_group", 7, 1), ("max_group", 8, 1), ("up", 5, -2), ("max_group", 9, 1), ("up", 6, -2),
    ("max_group", 10, 1), ("max_group", 11, 1), ("router", 0, -1), ("values_step", 2, 0), ("up", 7, -2),
    ("transpose_max", 0, 1), ("values_step", 3, 0), ("down", 1, -2), ("project_qk", 0, 2), ("up", 8, -2),
]
ACT_ORDER = [
    ("gap_exponential", 0, -4), ("copy_av", 0, -3), ("exp_group", 0, -2), ("exp_group", 1, -2),
    ("exp_group", 2, -2), ("exp_group", 3, -2), ("exp_group", 4, -2), ("exp_group", 5, -2),
    ("exp_group", 6, -2), ("exp_group", 7, -2), ("copy_attnT", 0, -3), ("exp_group", 8, -2),
    ("exp_group", 9, -2), ("exp_group", 10, -2), ("exp_group", 11, -2), ("copy_ckv", 0, 0), ("gelu", 0, -4),
    ("gelu", 1, -4), ("norm1", 0, -3), ("gelu", 2, -4), ("gelu", 3, -4), ("copy_xT", 0, 1),
    ("copy_hi_x1", 0, -3), ("gelu", 4, -4), ("gelu", 5, -4), ("gelu", 6, -4), ("copy_hi_max", 0, -1),
    ("gelu", 7, -4), ("copy_hi_qk", 0, 0), ("gelu", 8, -4),
]
DVE_ORDER = [
    ("split_x1", 0, -3), ("reduce_max", 7, -1), ("reduce_max", 8, -1), ("reduce_max", 9, -1),
    ("add_expert", 0, -4), ("reduce_max", 10, -1), ("reduce_max", 11, -1), ("route", 0, -3),
    ("split_max", 0, -1), ("add_expert", 1, -4), ("split_qk", 0, 0), ("add_expert", 2, -4), ("rotate", 0, 0),
    ("add_expert", 3, -4), ("normalise", 0, -2), ("add_expert", 4, -4), ("place_values", 0, 0),
    ("add_expert", 5, -4), ("make_gates", 0, -3), ("split_attnT", 0, -2), ("add_expert", 6, -4),
    ("residual1", 0, -2), ("add_expert", 7, -4), ("split_ckv", 0, 1), ("reduce_max", 0, 0),
    ("reduce_max", 1, 0), ("add_expert", 8, -4), ("reduce_max", 2, 0), ("moments2", 0, -4),
    ("reduce_max", 3, 0), ("reduce_max", 4, 0), ("reduce_max", 5, 0), ("reduce_max", 6, 0),
]
POOL_ORDER = [
    ("split_hidden", 2, -4), ("split_hidden", 3, -4), ("mask_group", 11, -2), ("split_hidden", 4, -4),
    ("split_hidden", 5, -4), ("split_hidden", 6, -4), ("split_hidden", 7, -4), ("split_hidden", 8, -4),
    ("split_rope", 0, 0), ("mask_group", 0, -1), ("mask_group", 1, -1), ("mask_group", 2, -1),
    ("mask_group", 3, -1), ("mask_group", 4, -1), ("mask_group", 5, -1), ("mask_group", 6, -1),
    ("mask_group", 7, -1), ("mask_group", 8, -1), ("mask_group", 9, -1), ("split_x", 0, 1),
    ("mask_group", 10, -1), ("deviation1", 0, -2), ("split_hidden", 0, -3), ("split_hidden", 1, -3),
    ("deviation2", 0, -4), ("norm2", 0, -4),
]
SP_ORDER = [
    ("stack_heads", 0, 0), ("stack_rope", 0, 0), ("load_x", 0, 2), ("load_residual", 0, 0), ("stack_max", 0, 0),
    ("store", 0, -4),
]


class Batch:

    def __init__(self, index, pair, parity):
        self.index, self.pair, self.parity = index, pair, parity
        self.exists = not isinstance(index, int) or 0 <= index < NB
        self.first = isinstance(index, int) and index == 0

    def count(self, per_batch, j=0):
        return self.index * per_batch + j

    def before(self, k):
        return Batch(self.index - k, None, (self.parity + k) % 2)


def walk(engine, iteration):

    def plain(i):
        def at(offset):
            n = i + offset
            return Batch(n, n // 2, n % 2)
        iteration(at)

    def looped(k, half):
        def at(offset):
            n = half + offset
            return Batch(2 * k + n, k + n // 2, n % 2)
        iteration(at)

    for i in range(-2, LOOP_FROM):
        plain(i)
    with engine.Fori(LOOP_FROM // 2, LOOP_TO // 2) as k:
        looped(k, 0)
        looped(k, 1)
    for i in range(LOOP_TO, NB + 4):
        plain(i)


def run(engine, order, steps):

    def iteration(at):
        for step, j, ahead in order:
            n = at(ahead)
            if n.exists:
                steps[step](n, j)

    walk(engine, iteration)


def wait(engine, semaphore, value):
    if not isinstance(value, int) or value > 0:
        engine.wait_ge(semaphore, value)


def wait_before(engine, semaphore, value, passed):
    if not isinstance(value, int) or value > 0:
        engine.wait_ge(semaphore, value)
        engine.sem_inc(passed, 1)


def av_of_group(g):
    return g // 2 if g < 8 else g - 4


def build_layer(nc, x, x_turned, w_attn, w_up, w_down, tables, q_rows, k_rows, out):
    ctx = ExitStack()
    with ctx:
        def sb(name, shape, dt=F32):
            return ctx.enter_context(nc.sbuf_tensor(name, shape, dt))

        def ps(name, shape):
            return ctx.enter_context(nc.psum_tensor(name, shape, F32))

        def sem(name):
            return ctx.enter_context(nc.semaphore(name))

        def parts(name, shape):
            return sb(f"{name}_hi", shape, F16), sb(f"{name}_lo", shape, F16)

        wa_in = sb("wa_in", [P, ATTN_COLS])
        wu_in = sb("wu_in", [P, NX, F])
        wd_in = sb("wd_in", [P, NX, NF, D])
        rope = sb("rope", [4 * DR, T])
        wa, wu, wd = parts("wa", [P, ATTN_COLS]), parts("wu", [P, NX, F]), parts("wd", [P, NX, NF, D])
        wkvd, wq, wk, wqr, wkr, wv, wo, wg = (
            [part[:, at:at + cols] for part in wa] for at, cols in zip(ATTN_AT, ATTN_WIDTHS))
        ident = sb("ident", [P, P])
        ident_bf = sb("ident_bf", [P, P], BF16)
        causal = sb("causal", [P, 4, BLOCK], BF16)
        minus_half = sb("minus_half", [P, NT])
        expert_no = sb("expert_no", [P, NE])
        expert_int = sb("expert_int", [P, NE], mybir.dt.int32)
        xT_in = sb("xT_in", [P, 2, T])
        xT = parts("xT", [P, 2, T])
        ckvT = parts("ckvT", [P, 2, T])
        qk = parts("qk", [P, 2, T])
        rope_cos = sb("rope_cos", [2 * DR, T])
        rope_sin = sb("rope_sin", [2 * DR, T])
        rope_sum = sb("rope_sum", [2 * DR, T])
        rope_hi, rope_lo = parts("roped", [2 * DR, T])
        q_st = sb("q_st", [P, 2, NH, T], F16)
        k_st = sb("k_st", [P, 2, NH, T], F16)
        v_pad = sb("v_pad", [P, 2, NT, NH, 32])
        neg_max = sb("neg_max", [P, NT, NH])
        nm_hi = sb("nm_hi", [NH, T], F16)
        nm_lo = sb("nm_lo", [NH, T], F16)
        probs = sb("probs", [P, N_GROUPS, 512])
        av_sb = sb("av_sb", [P, 2, T])
        sum_inv = sb("sum_inv", [P, NT, NH])
        attn = sb("attn", [P, NT, D])
        attnT = parts("attnT", [P, T])
        xres = sb("xres", [P, 2, NT, D])
        res1 = sb("res1", [P, NT, D])
        stats1 = sb("stats1", [P, NT, 6])
        mv1 = sb("mv1", [P, NT, 2])
        ve1 = sb("ve1", [P, NT])
        rstd1 = sb("rstd1", [P, NT])
        minus_mean1 = sb("minus_mean1", [P, NT])
        shift1 = sb("shift1", [P, NT])
        x1 = sb("x1", [P, 2, NT, D])
        x1T = parts("x1T", [P, 2, T])
        top = sb("top", [P, 2, NT, 8])
        top_at = sb("top_at", [P, 2, NT, 8], U32)
        logits = sb("logits", [P, NT, NE])
        gap = sb("gap", [P, 2, NT])
        gap_exp = sb("gap_exp", [P, NT])
        top_no = sb("top_no", [P, NT, 8])
        gate_den = sb("gate_den", [P, NT])
        gate = sb("gate", [P, NT, 2])
        pick = sb("pick", [P, 2, NT, NE])
        gates = sb("gates", [P, 2, NT, NE])
        hid_full = sb("hid_full", [P, NX, NF * T])
        hid = parts("hid", [P, NX, NF * T])
        acc = sb("acc", [P, NT, D])
        stats2 = sb("stats2", [P, NT, 6])
        mv2 = sb("mv2", [P, NT, 2])
        ve2 = sb("ve2", [P, NT])
        rstd2 = sb("rstd2", [P, NT])
        yout = sb("yout", [P, 2, NT, D])

        ring = ps("ring", [P, 3, 512])
        mbank = ps("mbank", [P, 2, 512])
        avbank = ps("avbank", [P, 2, T])
        xbank = ps("xbank", [P, 512])
        ybank = ps("ybank", [P, 512])

        ld_attn = sem("ld_attn")
        ld_rope = sem("ld_rope")
        ld_up = sem("ld_up")
        ld_down = sem("ld_down")
        st_mask = sem("st_mask")
        consts_made = sem("consts_made")
        dve_consts = sem("dve_consts")
        attn_hi = sem("attn_hi")
        attn_lo = sem("attn_lo")
        wide_hi = sem("wide_hi")
        wide_lo = sem("wide_lo")
        ld_x = [sem("ld_x0"), sem("ld_x1")]
        ld_r = [sem("ld_r0"), sem("ld_r1")]
        st_qk = sem("st_qk")
        st_rope = sem("st_rope")
        st_max = sem("st_max")
        st_out = [sem("st_out0"), sem("st_out1")]
        pe_ckv = sem("pe_ckv")
        pe_qk = sem("pe_qk")
        pe_rope = sem("pe_rope")
        pe_v = sem("pe_v")
        pe_max = sem("pe_max")
        pe_nmT = sem("pe_nmT")
        pe_score = sem("pe_score")
        pe_av = sem("pe_av")
        pe_avT = sem("pe_avT")
        pe_attnT = sem("pe_attnT")
        pe_o = sem("pe_o")
        pe_x1T = sem("pe_x1T")
        pe_logit = sem("pe_logit")
        pe_up = sem("pe_up")
        pe_down = sem("pe_down")
        act_xT = sem("act_xT")
        act_ckv = sem("act_ckv")
        act_qk_hi = sem("act_qk_hi")
        act_exp = sem("act_exp")
        act_av = sem("act_av")
        act_attnT = sem("act_attnT")
        act_x1_hi = sem("act_x1_hi")
        act_gap = sem("act_gap")
        act_nm_hi = sem("act_nm_hi")
        act_x1 = sem("act_x1")
        act_gelu = sem("act_gelu")
        pool_mask = sem("pool_mask")
        pool_hid = sem("pool_hid")
        pool_rstd1 = sem("pool_rstd1")
        pool_rstd2 = sem("pool_rstd2")
        pool_rope = sem("pool_rope")
        pool_out = sem("pool_out")
        pool_x_lo = sem("pool_x_lo")
        pool_passed = sem("pool_passed")
        dve_passed = sem("dve_passed")
        pe_passed = sem("pe_passed")
        sp_passed = sem("sp_passed")
        dve_ckv_lo = sem("dve_ckv_lo")
        dve_attnT_lo = sem("dve_attnT_lo")
        dve_qk_lo = sem("dve_qk_lo")
        dve_rope = sem("dve_rope")
        dve_v = sem("dve_v")
        dve_norm = sem("dve_norm")
        dve_ln1 = sem("dve_ln1")
        dve_x1_lo = sem("dve_x1_lo")
        dve_route = sem("dve_route")
        dve_gate = sem("dve_gate")
        dve_max = sem("dve_max")
        dve_nm = sem("dve_nm")
        dve_sum = sem("dve_sum")
        dve_ln2 = sem("dve_ln2")
        CONSTS = 6
        N_ROPE, N_V, N_NORM, N_LN, N_ROUTE, N_GATE = 2, 3, 5, 5, 6, 7
        N_SUM = 1 + NE * NT
        N_ROPE_SPLIT = 3
        N_LN2 = 2 * NT
        N_RSTD1 = 4

        x_tiles = x.rearrange("b (t p) d -> b p t d", p=P)
        out_tiles = out.rearrange("b (t p) d -> b p t d", p=P)

        def dram_batch(ap, batch):
            return ap[bass.ds(batch.index, 1)].rearrange("b p t d -> (b p) t d")

        def dram_turned(batch):
            return x_turned[bass.ds(batch.index, 1)].rearrange("b d t -> (b d) t")

        block = ctx.enter_context(nc.Block())

        @block.sync
        def _(sp):
            sp.dma_start(wa_in[:, :], w_attn).then_inc(ld_attn, 16)
            sp.dma_start(xT_in[:, 0], dram_turned(Batch(0, 0, 0))).then_inc(ld_x[0], 16)
            sp.dma_start(rope[:, :], tables).then_inc(ld_rope, 16)
            sp.dma_start(xT_in[:, 1], dram_turned(Batch(1, 0, 1))).then_inc(ld_x[1], 16)
            sp.dma_start(wu_in[:, :, :], w_up).then_inc(ld_up, 16)
            sp.dma_start(wd_in[:, :, :, :], w_down).then_inc(ld_down, 16)

            def load_x(n, _):
                if isinstance(n.index, int) and n.index < 2:
                    return
                wait_before(sp, pool_x_lo, n.count(1, -1), sp_passed)
                sp.dma_start(xT_in[:, n.parity], dram_turned(n)).then_inc(ld_x[n.parity], 16)

            def load_residual(n, _):
                wait_before(sp, dve_ln1, n.count(N_LN, 1 - 2 * N_LN), sp_passed)
                sp.dma_start(xres[:, n.parity], dram_batch(x_tiles, n)).then_inc(ld_r[n.parity], 16)

            def stack_heads(n, _):
                wait_before(sp, pe_score, n.count(N_GROUPS, -N_GROUPS), sp_passed)
                wait_before(sp, act_qk_hi, n.count(1, 1), sp_passed)
                wait_before(sp, dve_qk_lo, n.count(1, 1), sp_passed)
                for j, (q_part, k_part) in enumerate([(HI, HI), (HI, LO), (LO, HI)]):
                    rows = slice(ROPE_ROWS + j * HD, ROPE_ROWS + (j + 1) * HD)
                    sp.dma_start(q_st[rows, n.parity], qk[q_part][:, 0, :]).then_inc(st_qk, 16)
                    sp.dma_start(k_st[rows, n.parity], qk[k_part][:, 1, :]).then_inc(st_qk, 16)

            def stack_rope(n, _):
                wait_before(sp, pool_rope, n.count(N_ROPE_SPLIT, N_ROPE_SPLIT), sp_passed)
                for j, (q_part, k_part) in enumerate([(rope_hi, rope_hi), (rope_hi, rope_lo), (rope_lo, rope_hi)]):
                    for stack, part, at_row in [(q_st, q_part, 0), (k_st, k_part, DR)]:
                        src = part[at_row:at_row + DR, :].unsqueeze(1).to_broadcast([DR, NH, T])
                        sp.dma_start(stack[j * DR:(j + 1) * DR, n.parity], src).then_inc(st_rope, 16)

            def stack_max(n, _):
                wait_before(sp, dve_nm, n.count(1, 1), sp_passed)
                for j, part in enumerate([nm_hi, nm_lo]):
                    row = slice(MAX_ROWS + j, MAX_ROWS + j + 1)
                    sp.dma_start(q_st[row, n.parity], part[:, :]).then_inc(st_max, 16)

            def store(n, _):
                wait_before(sp, pool_out, n.count(NT, NT), sp_passed)
                sp.dma_start(dram_batch(out_tiles, n), yout[:, n.parity]).then_inc(st_out[n.parity], 16)

            for parity in range(2):
                for stack, rows in [(q_st, q_rows), (k_st, k_rows)]:
                    sp.dma_start(stack[QK_ROWS:QK_ROWS + rows.shape[0], parity],
                                 rows.unsqueeze(1).to_broadcast([rows.shape[0], NH, T])).then_inc(st_mask, 16)

            run(sp, SP_ORDER, {
                "load_x": load_x, "load_residual": load_residual, "stack_heads": stack_heads,
                "stack_rope": stack_rope, "store": store, "stack_max": stack_max,
            })
            for parity in range(2):
                sp.wait_ge(st_out[parity], 16 * NB // 2)

        @block.tensor
        def _(pe):
            def three(to, stationary, moving, start=True, stop=True, place=None):
                terms = [(HI, HI), (HI, LO), (LO, HI)]
                for j, (a, b) in enumerate(terms):
                    mm = pe.matmul(to, stationary[a][...], moving[b][...], start=start and j == 0, stop=stop and j == 2,
                                   tile_position=place)
                return mm

            def down_project(n):
                pe.wait_ge(pool_x_lo, n.count(1, 1))
                three(xbank[:, 0:T], wkvd, [part[:, n.parity, :] for part in xT]).then_inc(pe_ckv, 1)

            def project_qk(n):
                pe.wait_ge(dve_ckv_lo, n.count(1, 1))
                three(xbank[:, 0:T], wq,
                      [part[:, n.parity, :] for part in xT])
                three(xbank[:, T:2 * T], wk,
                      [part[:, n.parity, :] for part in ckvT]).then_inc(pe_qk, 1)

            def project_rope(n):
                for j, (a, b) in enumerate([(HI, HI), (HI, LO), (LO, HI)]):
                    for strip, (w, of, swapped) in enumerate(
                            [(wqr, xT, 0), (wkr, ckvT, 0), (wqr, xT, 1), (wkr, ckvT, 1)]):
                        mm = pe.matmul(xbank[DR * strip:DR * (strip + 1), 0:T],
                                       w[a][:, swapped * DR:(swapped + 1) * DR], of[b][:, n.parity, :],
                                       start=(j == 0), stop=(j == 2), tile_position=(0, DR * strip),
                                       skip_group_check=True)
                mm.then_inc(pe_rope, 1)

            def project_v(n):
                for t in range(NT):
                    mm = three(xbank[:, t * P:(t + 1) * P], [part[:, n.parity, t * P:(t + 1) * P] for part in ckvT], wv)
                mm.then_inc(pe_v, 1)

            def max_group(n, g):
                if n.first and g == 0:
                    pe.wait_ge(st_mask, 64)
                if g == 0:
                    pe.wait_ge(st_qk, n.count(96, 96))
                    pe.wait_ge(st_rope, n.count(96, 96))
                wait_before(pe, dve_max, n.count(N_GROUPS, g - 1), pe_passed)
                t, h0, nh = MAX_GROUPS[g]
                keys = (t + 1) * P
                bank = mbank[:, g % 2, :].rearrange("p (h k) -> p h k", h=nh)
                for strip in range(P // BLOCK):
                    rows = slice(strip * BLOCK, (strip + 1) * BLOCK)
                    at_key = t * P + strip * BLOCK
                    pe.matmul(bank[rows, :, at_key:at_key + BLOCK], ident_bf[rows, rows], causal[rows, 0:nh, :],
                              start=True, stop=False, tile_position=(rows.start, rows.start), skip_group_check=True)
                for a in range(nh):
                    mm = pe.matmul(bank[:, a, :], q_st[0:MAX_ROWS, n.parity, h0 + a, t * P:keys],
                                   k_st[0:MAX_ROWS, n.parity, h0 + a, 0:keys],
                                   start=False, stop=(a == nh - 1), skip_group_check=True)
                mm.then_inc(pe_max, 1)

            def transpose_max(n):
                pe.wait_ge(dve_max, n.count(N_GROUPS, N_GROUPS))
                for t in range(NT):
                    mm = pe.transpose(xbank[0:NH, t * P:(t + 1) * P], neg_max[:, t, :], ident[:, :])
                mm.then_inc(pe_nmT, 1)

            def score_group(n, g):
                if g == 0:
                    pe.wait_ge(st_max, n.count(32, 32))
                    pe.wait_ge(dve_v, n.count(N_V, N_V))
                if g >= 3:
                    pe.wait_ge(act_exp, n.count(N_GROUPS, g - 2))
                elif n.before(3).exists:
                    pe.wait_ge(act_gelu, n.before(3).count(NX, NX - 2 + g))
                else:
                    wait(pe, act_exp, n.count(N_GROUPS, g - 2))
                if g < 8:
                    heads, kt = QUADS[g // 2][2 * (g % 2):2 * (g % 2) + 2], 0
                else:
                    heads, kt = QUADS[g - 8], 1
                width = T - kt * P
                for a, h in enumerate(heads):
                    mm = pe.matmul(ring[:, g % 3, a * width:(a + 1) * width],
                                   k_st[0:STACK_ROWS, n.parity, h, kt * P:(kt + 1) * P],
                                   q_st[0:STACK_ROWS, n.parity, h, kt * P:T], start=True, stop=True)
                mm.then_inc(pe_score, 1)

            def values_step(n, s):
                groups = [2 * s, 2 * s + 1] if s < 4 else [s + 4]
                pe.wait_ge(pool_mask, n.count(N_GROUPS, groups[-1] + 1))
                if s == 0:
                    wait(pe, act_av, n.count(1, 0))
                kt, quad = s // 4, s % 4
                part, cols = quad // 3, slice(kt * P, T)
                for j, h in enumerate(QUADS[quad]):
                    if kt == 0:
                        p_cols = probs[:, groups[j // 2], (j % 2) * T:(j % 2 + 1) * T]
                    else:
                        p_cols = probs[:, groups[0], j * P:(j + 1) * P]
                    mm = pe.matmul(avbank[32 * j:32 * j + 32, part, cols], v_pad[:, n.parity, kt, h, :], p_cols,
                                   start=(s == 0), stop=(s == N_AV - 1), skip_group_check=True,
                                   tile_position=(0, 32 * j))
                mm.then_inc(pe_av, 1)

            def transpose_av(n):
                pe.wait_ge(act_av, n.count(1, 1))
                for part in range(2):
                    for t in range(NT):
                        mm = pe.transpose(xbank[:, (part * NT + t) * P:(part * NT + t + 1) * P],
                                          av_sb[:, part, t * P:(t + 1) * P], ident[:, :])
                mm.then_inc(pe_avT, 1)

            def transpose_attn(n):
                pe.wait_ge(dve_norm, n.count(N_NORM, N_NORM))
                for t in range(NT):
                    mm = pe.transpose(xbank[:, t * P:(t + 1) * P], attn[:, t, :], ident[:, :])
                mm.then_inc(pe_attnT, 1)

            def project_out(n):
                pe.wait_ge(dve_attnT_lo, n.count(1, 1))
                for t in range(NT):
                    mm = three(xbank[:, t * P:(t + 1) * P], [part[:, t * P:(t + 1) * P] for part in attnT], wo)
                mm.then_inc(pe_o, 1)

            def transpose_x1(n):
                pe.wait_ge(act_x1, n.count(1, 1))
                for t in range(NT):
                    mm = pe.transpose(xbank[:, t * P:(t + 1) * P], x1[:, n.parity, t, :], ident[:, :])
                mm.then_inc(pe_x1T, 1)

            def router(n):
                pe.wait_ge(dve_x1_lo, n.count(1, 1))
                for t in range(NT):
                    tokens = slice(t * P, (t + 1) * P)
                    mm = three(xbank[:, t * NE:(t + 1) * NE], [part[:, n.parity, tokens] for part in x1T], wg)
                mm.then_inc(pe_logit, 1)

            def up(n, e):
                if n.first and e == 0:
                    pe.wait_ge(wide_lo, 1)
                if e >= 3:
                    pe.wait_ge(act_gelu, n.count(NX, e - 2))
                elif n.before(-2).exists:
                    pe.wait_ge(act_exp, n.before(-2).count(N_GROUPS, N_GROUPS - 2 + e))
                else:
                    wait(pe, act_gelu, n.count(NX, e - 2))
                for c in range(NF):
                    mm = three(ring[:, e % 3, c * T:(c + 1) * T], [w[:, e, c * P:(c + 1) * P] for w in wu],
                               [part[:, n.parity, :] for part in x1T])
                mm.then_inc(pe_up, 1)

            def down(n, e):
                if n.first and e == 0:
                    pe.wait_ge(wide_lo, 2)
                pe.wait_ge(pool_hid, n.count(NX, e + 1))
                if e == 0:
                    wait(pe, dve_sum, n.count(N_SUM, 0))
                else:
                    pe.wait_ge(dve_sum, n.count(N_SUM, 1 + NT * (e - 1)))
                for t in range(NT):
                    for c in range(NF):
                        at_token = c * T + t * P
                        mm = three(ybank[:, t * D:(t + 1) * D], [part[:, e, at_token:at_token + P] for part in hid],
                                   [w[:, e, c, :] for w in wd], start=(c == 0), stop=(c == NF - 1))
                mm.then_inc(pe_down, 1)

            readers = {
                "down_project": (dve_ckv_lo, 1, 1), "project_qk": (dve_qk_lo, 1, 1),
                "project_rope": (dve_rope, N_ROPE, 2),
                "project_v": (dve_v, N_V, N_V), "transpose_av": (dve_norm, N_NORM, N_NORM),
                "transpose_attn": (dve_attnT_lo, 1, 1), "project_out": (dve_ln1, N_LN, 1),
                "transpose_x1": (dve_x1_lo, 1, 1), "router": (dve_route, N_ROUTE, 1), "transpose_max": (dve_nm, 1, 1),
            }
            sharing = [(step, ahead) for step, _, ahead in PE_ORDER if step in readers]

            def small(step, product):
                at_place = [other for other, _ in sharing].index(step)

                def taken(n, j):
                    for back in range(1, 4 * len(sharing)):
                        other, ahead = sharing[(at_place - back) % len(sharing)]
                        laps = (back - at_place + len(sharing) - 1) // len(sharing)
                        before = n.before(sharing[at_place][1] - ahead + laps)
                        if before.exists:
                            semaphore, per_batch, count = readers[other]
                            wait(pe, semaphore, before.count(per_batch, count))
                            break
                    product(n)
                return taken

            pe.wait_ge(consts_made, CONSTS)
            pe.wait_ge(attn_lo, 1)
            pe.wait_ge(dve_consts, 4)
            run(pe, PE_ORDER, {
                "down_project": small("down_project", down_project),
                "project_qk": small("project_qk", project_qk),
                "project_rope": small("project_rope", project_rope),
                "project_v": small("project_v", project_v),
                "transpose_av": small("transpose_av", transpose_av),
                "transpose_attn": small("transpose_attn", transpose_attn),
                "project_out": small("project_out", project_out),
                "transpose_x1": small("transpose_x1", transpose_x1),
                "router": small("router", router),
                "transpose_max": small("transpose_max", transpose_max),
                "max_group": max_group, "score_group": score_group, "values_step": values_step,
                "up": up, "down": down,
            })

        @block.scalar
        def _(act):
            act.wait_ge(ld_attn, 16)
            act.mul(wa[HI][:, :], wa_in[:, :], W_SCALE).then_inc(attn_hi, 1)

            def wide_weights():
                act.wait_ge(ld_up, 16)
                act.mul(wu[HI][:, :, :], wu_in[:, :, :], W_SCALE).then_inc(wide_hi, 1)
                act.wait_ge(ld_down, 16)
                act.mul(wd[HI][:, :, :, :], wd_in[:, :, :, :], W_SCALE).then_inc(wide_hi, 1)

            def copy_hi_qk(n, _):
                act.wait_ge(pe_qk, n.count(1, 1))
                wait(act, st_qk, n.count(96, 0))
                act.mul(qk[HI][:, :, :].rearrange("p a t -> p (a t)"), xbank[:, :], 1.0 / W_SCALE
                        ).then_inc(act_qk_hi, 1)

            def gap_exponential(n, _):
                act.wait_ge(dve_route, n.count(N_ROUTE, N_ROUTE))
                wait(act, dve_gate, n.count(N_GATE, 0))
                act.activation(gap_exp[:, :], gap[:, n.parity, :], ACT.Exp, scale=UNSCALE).then_inc(act_gap, 1)

            def exp_group(n, g):
                if n.first and g == 0:
                    wide_weights()
                act.wait_ge(pe_score, n.count(N_GROUPS, g + 1))
                wait(act, pe_av, n.count(N_AV, av_of_group(g) + 1 - N_AV))
                act.activation(probs[:, g, :], ring[:, g % 3, :], ACT.Exp, scale=SCORE_SCALE
                               ).then_inc(act_exp, 1)

            def copy_av(n, _):
                act.wait_ge(pe_av, n.count(N_AV, N_AV))
                wait(act, pe_avT, n.count(1, 0))
                act.copy(av_sb[:, :, :], avbank[:, :, :]).then_inc(act_av, 1)

            def copy_attnT(n, _):
                act.wait_ge(pe_attnT, n.count(1, 1))
                wait(act, pe_o, n.count(1, 0))
                act.copy(attnT[HI][:, :], xbank[:, 0:T]).then_inc(act_attnT, 1)

            def copy_xT(n, _):
                act.wait_ge(ld_x[n.parity], n.pair * 16 + 16)
                wait(act, pe_qk, n.count(1, -1))
                wait(act, pe_rope, n.count(1, -1))
                act.copy(xT[HI][:, n.parity, :], xT_in[:, n.parity, :]).then_inc(act_xT, 1)

            def copy_ckv(n, _):
                act.wait_ge(pe_ckv, n.count(1, 1))
                wait(act, pe_qk, n.count(1, -1))
                wait(act, pe_rope, n.count(1, -1))
                wait(act, pe_v, n.count(1, -1))
                act.mul(ckvT[HI][:, n.parity, :], xbank[:, 0:T], 1.0 / W_SCALE).then_inc(act_ckv, 1)

            def copy_hi_x1(n, _):
                act.wait_ge(pe_x1T, n.count(1, 1))
                wait(act, pe_up, n.count(NX, -NX))
                act.mul(x1T[HI][:, n.parity, :], xbank[:, 0:T], X_SCALE).then_inc(act_x1_hi, 1)

            def copy_hi_max(n, _):
                act.wait_ge(pe_nmT, n.count(1, 1))
                wait(act, st_max, n.count(32, 0))
                act.copy(nm_hi[:, :], xbank[0:NH, 0:T]).then_inc(act_nm_hi, 1)

            def norm1(n, _):
                act.wait_ge(pool_rstd1, n.count(N_RSTD1, N_RSTD1))
                wait(act, dve_sum, n.count(N_SUM, 1 - 2 * N_SUM))
                for t in range(NT):
                    done = act.activation(x1[:, n.parity, t, :], res1[:, t, :], ACT.Identity, scale=rstd1[:, t:t + 1],
                                          bias=shift1[:, t:t + 1])
                done.then_inc(act_x1, 1)

            def gelu(n, e):
                act.wait_ge(pe_up, n.count(NX, e + 1))
                wait(act, pe_down, n.count(NX, e + 1 - NX))
                act.activation(hid[HI][:, e, :], ring[:, e % 3, :], ACT.Gelu, scale=UNSCALE)
                wait(act, pool_hid, n.count(NX, e + 1 - NX))
                act.activation(hid_full[:, e, :], ring[:, e % 3, :], ACT.Gelu, scale=UNSCALE
                               ).then_inc(act_gelu, 1)

            run(act, ACT_ORDER, {
                "copy_xT": copy_xT, "copy_ckv": copy_ckv, "copy_hi_qk": copy_hi_qk, "exp_group": exp_group,
                "copy_av": copy_av, "copy_attnT": copy_attnT, "copy_hi_x1": copy_hi_x1,
                "gap_exponential": gap_exponential, "gelu": gelu, "copy_hi_max": copy_hi_max, "norm1": norm1,
            })

        @block.gpsimd
        def _(pool):
            pool.memset(ident[:, :], 0.0).then_inc(consts_made, 1)
            pool.wait_ge(consts_made, 1)
            pool.affine_select(out=ident[:, :], in_=ident[:, :], compare_op=ALU.not_equal, fill=1.0, base=0,
                               pattern=[[-1, P]], channel_multiplier=1).then_inc(consts_made, 1)
            pool.wait_ge(consts_made, 2)
            pool.memset(causal[:, :, :], 0.0).then_inc(consts_made, 1)
            pool.wait_ge(consts_made, 3)
            for strip in range(P // BLOCK):
                rows = slice(strip * BLOCK, (strip + 1) * BLOCK)
                masked = pool.affine_select(out=causal[rows, :, :], in_=causal[rows, :, :], compare_op=ALU.is_ge,
                                            fill=NEG, base=0, pattern=[[0, 4], [-1, BLOCK]], channel_multiplier=1)
            masked.then_inc(consts_made, 1)
            pool.wait_ge(consts_made, 4)
            pool.memset(minus_half[:, :], -0.5).then_inc(consts_made, 1)
            pool.wait_ge(consts_made, 5)
            pool.iota(expert_int[:, :], pattern=[[1, NE]], base=0, channel_multiplier=0).then_inc(consts_made, 1)
            pool.wait_ge(consts_made, CONSTS)

            def mask_group(n, g):
                wait_before(pool, act_exp, n.count(N_GROUPS, g + 1), pool_passed)
                heads = 2 if g < 8 else 4
                block_of = probs[:, g, :].rearrange("p (a q) -> p a q", a=heads)[:, :, 0:P]
                pool.affine_select(out=block_of, in_=block_of, compare_op=ALU.is_ge, fill=0.0, base=0,
                                   pattern=[[0, heads], [1, P]], channel_multiplier=-1).then_inc(pool_mask, 1)

            def split_hidden(n, e):
                pool.wait_ge(act_gelu, n.count(NX, e + 1))
                wait(pool, pe_down, n.count(NX, e + 1 - NX))
                pool.tensor_tensor(hid[LO][:, e, :], hid_full[:, e, :], hid[HI][:, e, :], ALU.subtract
                                   ).then_inc(pool_hid, 1)

            def split_x(n, _):
                pool.wait_ge(act_xT, n.count(1, 1))
                pool.tensor_tensor(xT[LO][:, n.parity, :], xT_in[:, n.parity, :], xT[HI][:, n.parity, :], ALU.subtract
                                   ).then_inc(pool_x_lo, 1)

            def split_rope(n, _):
                pool.wait_ge(dve_rope, n.count(N_ROPE, N_ROPE))
                pool.tensor_tensor(rope_sum[:, :], rope_cos[:, :], rope_sin[:, :], ALU.add).then_inc(pool_rope, 1)
                wait(pool, st_rope, n.count(96, 0))
                wait_before(pool, pool_rope, n.count(N_ROPE_SPLIT, 1), pool_passed)
                pool.tensor_copy(rope_hi[:, :], rope_sum[:, :]).then_inc(pool_rope, 1)
                pool.wait_ge(pool_rope, n.count(N_ROPE_SPLIT, 2))
                pool.tensor_tensor(rope_lo[:, :], rope_sum[:, :], rope_hi[:, :], ALU.subtract).then_inc(pool_rope, 1)

            def inverse_deviation(n, made, mv, ve, rstd, done, per_batch=2):
                wait_before(pool, made[0], made[1], pool_passed)
                pool.tensor_scalar(ve[:, :], mv[:, :, 1], EPS, None, ALU.add).then_inc(done, 1)
                pool.wait_ge(done, n.count(per_batch, 1))
                pool.tensor_tensor(rstd[:, :], ve[:, :], minus_half[:, :], ALU.pow).then_inc(done, 1)

            def deviation1(n, _):
                inverse_deviation(n, (dve_ln1, n.count(N_LN, N_LN)), mv1, ve1, rstd1, pool_rstd1, N_RSTD1)
                wait_before(pool, pool_rstd1, n.count(N_RSTD1, 2), pool_passed)
                pool.tensor_scalar(minus_mean1[:, :], mv1[:, :, 0], -1.0, None, ALU.mult).then_inc(pool_rstd1, 1)
                pool.wait_ge(pool_rstd1, n.count(N_RSTD1, 3))
                pool.tensor_tensor(shift1[:, :], minus_mean1[:, :], rstd1[:, :], ALU.mult).then_inc(pool_rstd1, 1)

            def deviation2(n, _):
                inverse_deviation(n, (dve_ln2, n.count(N_LN2, N_LN2)), mv2, ve2, rstd2, pool_rstd2)

            def norm2(n, _):
                wait(pool, st_out[n.parity], n.pair * 16)
                wait_before(pool, pool_rstd2, n.count(2, 2), pool_passed)
                for t in range(NT):
                    pool.tensor_scalar(yout[:, n.parity, t, :], acc[:, t, :], mv2[:, t, 0:1], rstd2[:, t:t + 1],
                                       ALU.subtract, ALU.mult).then_inc(pool_out, 1)

            run(pool, POOL_ORDER, {
                "mask_group": mask_group, "split_hidden": split_hidden, "deviation1": deviation1,
                "deviation2": deviation2, "norm2": norm2, "split_x": split_x, "split_rope": split_rope,
            })

        @block.vector
        def _(dve):
            dve.memset(v_pad[:, :, :, :, :], 0.0).then_inc(dve_consts, 1)
            dve.wait_ge(dve_consts, 1)
            for parity in range(2):
                for t in range(NT):
                    for quad, heads in enumerate(QUADS):
                        at_col = 9 * quad + SUMCOL if quad < 3 else SUMCOL
                        step = heads[1] - heads[0]
                        ones = dve.memset(v_pad[:, parity, t, heads[0]:heads[3] + 1:step, at_col:at_col + 1], 1.0)
            ones.then_inc(dve_consts, 1)
            dve.wait_ge(consts_made, CONSTS)
            dve.tensor_copy(ident_bf[:, :], ident[:, :]).then_inc(dve_consts, 1)
            dve.tensor_copy(expert_no[:, :], expert_int[:, :]).then_inc(dve_consts, 1)
            dve.wait_ge(attn_hi, 1)
            dve.scalar_tensor_tensor(wa[LO][:, :], wa_in[:, :], W_SCALE, wa[HI][:, :], ALU.mult, ALU.subtract
                                     ).then_inc(attn_lo, 1)

            def wide_weights():
                dve.wait_ge(wide_hi, 1)
                dve.scalar_tensor_tensor(wu[LO][:, :, :], wu_in[:, :, :], W_SCALE, wu[HI][:, :, :], ALU.mult,
                                         ALU.subtract).then_inc(wide_lo, 1)
                dve.wait_ge(wide_hi, 2)
                dve.scalar_tensor_tensor(wd[LO][:, :, :, :], wd_in[:, :, :, :], W_SCALE, wd[HI][:, :, :, :], ALU.mult,
                                         ALU.subtract).then_inc(wide_lo, 1)

            def low_part(lo, hi, of, scale, done):
                dve.scalar_tensor_tensor(lo, of, scale, hi, ALU.mult, ALU.subtract).then_inc(done, 1)

            def split_ckv(n, _):
                dve.wait_ge(act_ckv, n.count(1, 1))
                low_part(ckvT[LO][:, n.parity, :], ckvT[HI][:, n.parity, :], xbank[:, 0:T], 1.0 / W_SCALE, dve_ckv_lo)

            def split_attnT(n, _):
                dve.wait_ge(act_attnT, n.count(1, 1))
                low_part(attnT[LO][:, :], attnT[HI][:, :], xbank[:, 0:T], 1.0, dve_attnT_lo)

            def split_qk(n, _):
                dve.wait_ge(act_qk_hi, n.count(1, 1))
                wait(dve, st_qk, n.count(96, 0))
                low_part(qk[LO][:, :, :].rearrange("p a t -> p (a t)"), qk[HI][:, :, :].rearrange("p a t -> p (a t)"),
                         xbank[:, :], 1.0 / W_SCALE, dve_qk_lo)

            def rotate(n, _):
                if n.first:
                    dve.wait_ge(ld_rope, 16)
                dve.wait_ge(pe_rope, n.count(1, 1))
                plain, swapped = slice(0, 2 * DR), slice(2 * DR, 4 * DR)
                wait(dve, pool_rope, n.count(N_ROPE_SPLIT, 1 - N_ROPE_SPLIT))
                dve.tensor_tensor(rope_cos[:, :], xbank[plain, 0:T], rope[plain, :], ALU.mult).then_inc(dve_rope, 1)
                dve.tensor_tensor(rope_sin[:, :], xbank[swapped, 0:T], rope[swapped, :], ALU.mult).then_inc(dve_rope, 1)

            def place_values(n, _):
                dve.wait_ge(pe_v, n.count(1, 1))
                wait(dve, pe_av, n.count(N_AV, -N_AV))
                for t in range(NT):
                    to = v_pad[:, n.parity, t, :, :].rearrange("p h c -> p (h c)")
                    v = xbank[:, t * P:(t + 1) * P]
                    dst = bass.AP(to.tensor, to.offset, [list(to.ap[0]), [96, 4], [41, 3], [1, HD]])
                    dve.tensor_scalar(dst, v[:, 0:12 * HD].rearrange("p (j i d) -> p j i d", j=4, i=3),
                                      1.0 / W_SCALE, None, ALU.mult).then_inc(dve_v, 1)
                v = xbank[:, 0:NT * P].rearrange("p (t h d) -> p t h d", t=NT, d=HD)
                dve.tensor_scalar(v_pad[:, n.parity, :, 12:NH, 0:HD], v[:, :, 12:NH, :], 1.0 / W_SCALE, None,
                                  ALU.mult).then_inc(dve_v, 1)

            def normalise(n, _):
                if n.first:
                    wide_weights()
                dve.wait_ge(pe_avT, n.count(1, 1))
                a = xbank[:, 0:NT * P].rearrange("p (t j c) -> p t j c", t=NT, j=4)
                b = xbank[:, NT * P:2 * NT * P].rearrange("p (t j c) -> p t j c", t=NT, j=4)
                dve.reciprocal(sum_inv[:, :, 0:12].rearrange("p t (j i) -> p t j i", j=4),
                               a[:, :, :, SUMCOL:27:9]).then_inc(dve_norm, 1)
                dve.reciprocal(sum_inv[:, :, 12:NH].unsqueeze(3), b[:, :, :, SUMCOL:SUMCOL + 1]).then_inc(dve_norm, 1)
                dve.wait_ge(dve_norm, n.count(N_NORM, 2))
                for t in range(NT):
                    dve.tensor_tensor(
                        attn[:, t, 0:12 * HD].rearrange("p (j i d) -> p j i d", j=4, i=3),
                        a[:, t, :, 0:27].rearrange("p j (i c) -> p j i c", c=9)[:, :, :, 0:HD],
                        sum_inv[:, t, 0:12].rearrange("p (j i) -> p j i", j=4).unsqueeze(3).to_broadcast([P, 4, 3, HD]),
                        ALU.mult).then_inc(dve_norm, 1)
                dve.tensor_tensor(attn[:, :, 12 * HD:D].rearrange("p t (j d) -> p t j d", d=HD), b[:, :, :, 0:HD],
                                  sum_inv[:, :, 12:NH].unsqueeze(3).to_broadcast([P, NT, 4, HD]),
                                  ALU.mult).then_inc(dve_norm, 1)

            def moments(n, of, stats, mv, done, per_batch, first):
                dve.wait_ge(done, n.count(per_batch, first))
                for t in range(NT):
                    dve.bn_stats(stats[:, t, :], of[:, t, :]).then_inc(done, 1)
                wait_before(dve, done, n.count(per_batch, first + NT), dve_passed)
                for t in range(NT):
                    dve.bn_aggr(mv[:, t, :], stats[:, t, :]).then_inc(done, 1)

            def residual1(n, _):
                dve.wait_ge(pe_o, n.count(1, 1))
                wait(dve, act_x1, n.count(1, 0))
                dve.wait_ge(ld_r[n.parity], n.pair * 16 + 16)
                dve.scalar_tensor_tensor(res1[:, :, :].rearrange("p t d -> p (t d)"), xbank[:, 0:T], 1.0 / W_SCALE,
                                         xres[:, n.parity, :, :].rearrange("p t d -> p (t d)"),
                                         ALU.mult, ALU.add).then_inc(dve_ln1, 1)
                moments(n, res1, stats1, mv1, dve_ln1, N_LN, 1)

            def split_x1(n, _):
                dve.wait_ge(act_x1_hi, n.count(1, 1))
                low_part(x1T[LO][:, n.parity, :], x1T[HI][:, n.parity, :], xbank[:, 0:T], X_SCALE, dve_x1_lo)

            def route(n, _):
                dve.wait_ge(pe_logit, n.count(1, 1))
                dve.tensor_copy(logits[:, :, :].rearrange("p t e -> p (t e)"), xbank[:, 0:NT * NE]
                                ).then_inc(dve_route, 1)
                wait_before(dve, dve_route, n.count(N_ROUTE, 1), dve_passed)
                for t in range(NT):
                    dve.max(top[:, n.parity, t, :], logits[:, t, :]).then_inc(dve_route, 1)
                wait_before(dve, dve_route, n.count(N_ROUTE, 3), dve_passed)
                for t in range(NT):
                    dve.max_index(top_at[:, n.parity, t, :], top[:, n.parity, t, :], logits[:, t, :]
                                  ).then_inc(dve_route, 1)
                dve.tensor_tensor(gap[:, n.parity, :], top[:, n.parity, :, 1], top[:, n.parity, :, 0], ALU.subtract
                                  ).then_inc(dve_route, 1)

            def make_gates(n, _):
                dve.wait_ge(act_gap, n.count(1, 1))
                dve.tensor_copy(top_no[:, :, :], top_at[:, n.parity, :, :]).then_inc(dve_gate, 1)
                dve.tensor_scalar(gate_den[:, :], gap_exp[:, :], 1.0, W_SCALE, ALU.add, ALU.mult).then_inc(dve_gate, 1)
                dve.wait_ge(dve_gate, n.count(N_GATE, 2))
                dve.reciprocal(gate[:, :, 0], gate_den[:, :]).then_inc(dve_gate, 1)
                dve.wait_ge(dve_gate, n.count(N_GATE, 3))
                dve.tensor_tensor(gate[:, :, 1], gap_exp[:, :], gate[:, :, 0], ALU.mult).then_inc(dve_gate, 1)
                dve.wait_ge(dve_gate, n.count(N_GATE, 4))
                picked = pick[:, :, :, :].rearrange("p j t e -> p t j e")
                dve.tensor_tensor(picked, expert_no[:, :].unsqueeze(1).unsqueeze(1).to_broadcast([P, NT, 2, NE]),
                                  top_no[:, :, 0:2].unsqueeze(3).to_broadcast([P, NT, 2, NE]), ALU.is_equal
                                  ).then_inc(dve_gate, 1)
                dve.wait_ge(dve_gate, n.count(N_GATE, 5))
                dve.tensor_tensor(picked, picked, gate[:, :, :].unsqueeze(3).to_broadcast([P, NT, 2, NE]), ALU.mult
                                  ).then_inc(dve_gate, 1)
                dve.wait_ge(dve_gate, n.count(N_GATE, 6))
                dve.tensor_tensor(gates[:, n.parity, :, :], pick[:, 0, :, :], pick[:, 1, :, :], ALU.add
                                  ).then_inc(dve_gate, 1)

            def reduce_max(n, g):
                dve.wait_ge(pe_max, n.count(N_GROUPS, g + 1))
                if g == 0:
                    wait(dve, pe_nmT, n.count(1, 0))
                t, h0, nh = MAX_GROUPS[g]
                dve.tensor_reduce(neg_max[:, t, h0:h0 + nh], mbank[:, g % 2, :].rearrange("p (h k) -> p h k", h=nh),
                                  AX_X, ALU.max, negate=True).then_inc(dve_max, 1)

            def split_max(n, _):
                dve.wait_ge(act_nm_hi, n.count(1, 1))
                dve.tensor_tensor(nm_lo[:, :], xbank[0:NH, 0:T], nm_hi[:, :], ALU.subtract).then_inc(dve_nm, 1)

            def add_expert(n, e):
                dve.wait_ge(pe_down, n.count(NX, e + 1))
                if e == 0:
                    wait(dve, pool_out, n.count(NT, 0))
                    dve.scalar_tensor_tensor(acc[:, :, :].rearrange("p t d -> p (t d)"), ybank[:, 0:T], 1.0 / W_SCALE,
                                             x1[:, n.parity, :, :].rearrange("p t d -> p (t d)"),
                                             ALU.mult, ALU.add).then_inc(dve_sum, 1)
                    return
                if e == 1:
                    dve.wait_ge(dve_gate, n.count(N_GATE, N_GATE))
                dve.wait_ge(dve_sum, n.count(N_SUM, 1 + NT * (e - 1)))
                for t in range(NT):
                    dve.scalar_tensor_tensor(acc[:, t, :], ybank[:, t * D:(t + 1) * D],
                                             gates[:, n.parity, t, e - 1:e], acc[:, t, :], ALU.mult, ALU.add
                                             ).then_inc(dve_sum, 1)

            def moments2(n, _):
                dve.wait_ge(dve_sum, n.count(N_SUM, N_SUM))
                for t in range(NT):
                    dve.bn_stats(stats2[:, t, :], acc[:, t, :]).then_inc(dve_ln2, 1)
                wait_before(dve, dve_ln2, n.count(N_LN2, NT), dve_passed)
                for t in range(NT):
                    dve.bn_aggr(mv2[:, t, :], stats2[:, t, :]).then_inc(dve_ln2, 1)

            run(dve, DVE_ORDER, {
                "split_ckv": split_ckv, "split_attnT": split_attnT,
                "split_qk": split_qk, "rotate": rotate, "place_values": place_values, "reduce_max": reduce_max,
                "split_max": split_max, "normalise": normalise, "residual1": residual1,
                "split_x1": split_x1, "route": route, "make_gates": make_gates, "add_expert": add_expert,
                "moments2": moments2
            })


def rope_tables():
    exponent = np.arange(0, DR, 2, dtype=np.float32) / np.float32(DR)
    inv_freq = (1.0 / np.float32(10000.0) ** exponent).astype(np.float32)
    angle = np.outer(np.arange(T, dtype=np.float32), inv_freq).astype(np.float32).T
    cos = np.concatenate([np.cos(angle), np.cos(angle)])
    sin = np.concatenate([-np.sin(angle), np.sin(angle)])
    both = np.concatenate([cos, cos, sin, sin]) / W_SCALE
    return np.ascontiguousarray(both.astype(np.float32))


def stack_rows():
    big = 60000.0
    own = [b for b in range(T // BLOCK) if (b + 1) % (P // BLOCK)]
    block = np.arange(T) // BLOCK
    q_rows = np.stack([np.where(block == b, big, 0.0) for b in own])
    k_rows = np.stack([np.where(block > b, -big, 0.0) for b in own] + [np.ones(T), np.ones(T)])
    return {"q_rows": q_rows.astype(np.float16), "k_rows": k_rows.astype(np.float16)}


def weights_laid_out(inputs):
    attn = {name: np.asarray(inputs[f"L0_attn_W_{name}"])
            for name in ["kv_down", "k_up", "v_up", "q", "q_rope", "k_rope", "o"]}

    def by_place(w):
        return w.reshape(P, NH, HD).transpose(0, 2, 1).reshape(P, D)

    def with_swapped(w):
        return np.concatenate([w, w[:, DR // 2:], w[:, :DR // 2]], axis=1)

    narrow = [attn["kv_down"], by_place(attn["q"]), by_place(attn["k_up"]), with_swapped(attn["q_rope"]),
              with_swapped(attn["k_rope"]), attn["v_up"], attn["o"], inputs["L0_ffn_Wg"]]
    up = np.concatenate([inputs["L0_ffn_W1"][None], inputs["L0_ffn_Wu"]])
    down = np.concatenate([inputs["L0_ffn_W2"][None], inputs["L0_ffn_Wd"]])
    return {
        "w_attn": np.ascontiguousarray(np.concatenate(narrow, axis=1)),
        "w_up": np.ascontiguousarray(up.transpose(1, 0, 2)),
        "w_down": np.ascontiguousarray(down.reshape(NX, NF, P, D).transpose(2, 0, 1, 3)),
    }


def kernel(**inputs):
    import concourse.bacc as bacc
    from concourse.bass_utils import run_bass_kernel_spmd

    nc = bacc.Bacc("TRN2", target_bir_lowering=False, num_devices=1)
    x = np.ascontiguousarray(inputs["L0_attn_x"])
    arrays = {"x": x, "x_turned": np.ascontiguousarray(x.transpose(0, 2, 1)), **weights_laid_out(inputs),
              "rope_tables": rope_tables(), **stack_rows()}
    args = [nc.dram_tensor(name, a.shape, mybir.dt.from_np(a.dtype), kind="ExternalInput").ap()
            for name, a in arrays.items()]
    out = nc.dram_tensor("out", (NB, T, D), F32, kind="ExternalOutput").ap()
    build_layer(nc, *args, out)
    r = run_bass_kernel_spmd(nc, [arrays], core_ids=[0])
    return r.results[0]["out"]
```
